# Optimizing a Trainium2 kernel written in Bass

```python
import numpy as np
import jax
import jax.numpy as jnp

def _softmax(x, axis=-1):
    return jax.nn.softmax(x, axis=axis)

def _gelu(x):
    return jax.nn.gelu(x, approximate=True)

def _silu(x):
    return jax.nn.silu(x)

def _sigmoid(x):
    return jax.nn.sigmoid(x)

def _layernorm(x, axis=-1, eps=1e-05):
    m = jnp.mean(x, axis=axis, keepdims=True)
    v = jnp.var(x, axis=axis, keepdims=True)
    return (x - m) / jnp.sqrt(v + eps)

def _scatter_add(tgt, idx, src, axis=0):
    return tgt.at[idx].add(src)

def _segment_sum(src, seg, n):
    return jax.ops.segment_sum(src, seg, n)
kernel_name = 'mk_adj_preln_d1_adj_r2_758b52'

def setup_inputs(seed: int=0):
    np.random.seed(seed)
    _w = jnp.asarray

    def _rec_inputs():
        import jax
        import jax.numpy as jnp
        _gk = jax.random.key(seed)
        x = -0.0002928 + 1 * jax.random.normal(jax.random.fold_in(_gk, 1), (64, 128, 256), jnp.float32)
        _a = jax.random.bernoulli(jax.random.fold_in(_gk, 2), 0.125, (64, 128, 128))
        _a = jnp.logical_or(_a, jnp.swapaxes(_a, -1, -2))
        _a = jnp.logical_or(_a, jnp.eye(128, dtype=bool))
        adj = _a.astype(jnp.int32)
        return (x, adj)
    x, adj = _rec_inputs()

    def _L0_gnn_setup():
        import jax, jax.numpy as jnp
        import numpy as np
        L = 3
        D = 256
        B, N = (8, 512)
        EPS = 1e-05

        def layernorm(x, gamma, beta):
            mu = jnp.mean(x, axis=-1, keepdims=True)
            var = jnp.var(x, axis=-1, keepdims=True)
            return (x - mu) * jax.lax.rsqrt(var + EPS) * gamma + beta
        key = jax.random.key(seed)
        ks = jax.random.split(key, 12)
        s = 1.0 / np.sqrt(D)
        node_features = jax.random.normal(ks[0], (B, N, D), dtype=jnp.float32)
        adjacency_matrix = jax.random.randint(ks[1], (B, N, N), 0, 2, dtype=jnp.int32)
        return {'node_features': node_features, 'adjacency_matrix': adjacency_matrix, 'attn_w': jax.random.normal(ks[2], (L, 2 * D), dtype=jnp.float32) * (1.0 / np.sqrt(2 * D)), 'attn_b': jax.random.normal(ks[3], (L,), dtype=jnp.float32) * 0.01, 'W1': jax.random.normal(ks[4], (L, D, 4 * D), dtype=jnp.float32) * s, 'b1': jnp.zeros((L, 4 * D), dtype=jnp.float32), 'W2': jax.random.normal(ks[5], (L, 4 * D, D), dtype=jnp.float32) * (1.0 / np.sqrt(4 * D)), 'b2': jnp.zeros((L, D), dtype=jnp.float32), 'g1': jnp.ones((L, D), dtype=jnp.float32), 'beta1': jnp.zeros((L, D), dtype=jnp.float32), 'g2': jnp.ones((L, D), dtype=jnp.float32), 'beta2': jnp.zeros((L, D), dtype=jnp.float32)}
    _L0_gnn_all = _L0_gnn_setup()
    _L0_gnn_in = {k: v for k, v in _L0_gnn_all.items() if k in ('attn_w', 'attn_b', 'W1', 'b1', 'W2', 'b2', 'g1', 'beta1', 'g2', 'beta2')}
    del _L0_gnn_all
    return {'x': x, 'adj': adj, 'L0_gnn_attn_w': _L0_gnn_in['attn_w'], 'L0_gnn_attn_b': _L0_gnn_in['attn_b'], 'L0_gnn_W1': _L0_gnn_in['W1'], 'L0_gnn_b1': _L0_gnn_in['b1'], 'L0_gnn_W2': _L0_gnn_in['W2'], 'L0_gnn_b2': _L0_gnn_in['b2'], 'L0_gnn_g1': _L0_gnn_in['g1'], 'L0_gnn_beta1': _L0_gnn_in['beta1'], 'L0_gnn_g2': _L0_gnn_in['g2'], 'L0_gnn_beta2': _L0_gnn_in['beta2']}

def reference(x, adj, L0_gnn_attn_w, L0_gnn_attn_b, L0_gnn_W1, L0_gnn_b1, L0_gnn_W2, L0_gnn_b2, L0_gnn_g1, L0_gnn_beta1, L0_gnn_g2, L0_gnn_beta2):
    import jax
    import jax.numpy as jnp

    def _L0_gnn_ref(node_features, adjacency_matrix, attn_w, attn_b, W1, b1, W2, b2, g1, beta1, g2, beta2):
        import jax, jax.numpy as jnp
        import numpy as np
        L = 3
        D = 256
        B, N = (8, 512)
        EPS = 1e-05

        def layernorm(x, gamma, beta):
            mu = jnp.mean(x, axis=-1, keepdims=True)
            var = jnp.var(x, axis=-1, keepdims=True)
            return (x - mu) * jax.lax.rsqrt(var + EPS) * gamma + beta
        n = adjacency_matrix.shape[-1]
        mask = adjacency_matrix.astype(jnp.float32) + jnp.eye(n, dtype=jnp.float32) > 0
        x = node_features
        d = x.shape[-1]
        for l in range(attn_w.shape[0]):
            si = x @ attn_w[l, :d]
            sj = x @ attn_w[l, d:]
            scores = si[:, :, None] + sj[:, None, :] + attn_b[l]
            scores = jnp.where(scores >= 0, scores, 0.2 * scores)
            scores = jnp.where(mask, scores, -jnp.inf)
            attn = jax.nn.softmax(scores, axis=-1)
            agg = jnp.einsum('bij,bjd->bid', attn, x)
            h = layernorm(x + agg, g1[l], beta1[l])
            ff = jax.nn.gelu(h @ W1[l] + b1[l], approximate=False) @ W2[l] + b2[l]
            x = layernorm(h + ff, g2[l], beta2[l])
        return x
    h = jnp.maximum(_layernorm(x, axis=-1), 0.0)
    x = x + _L0_gnn_ref(h, adj, L0_gnn_attn_w, L0_gnn_attn_b, L0_gnn_W1, L0_gnn_b1, L0_gnn_W2, L0_gnn_b2, L0_gnn_g1, L0_gnn_beta1, L0_gnn_g2, L0_gnn_beta2)
    return x

_drawn_inputs = setup_inputs


def setup_inputs(seed=0):
    import zlib

    import numpy as np

    out = dict(_drawn_inputs(seed))
    spreads = {'L0_gnn_b1': (0.0, 0.1),
     'L0_gnn_b2': (0.0, 0.1),
     'L0_gnn_g1': (1.0, 0.2),
     'L0_gnn_beta1': (0.0, 0.1),
     'L0_gnn_g2': (1.0, 0.2),
     'L0_gnn_beta2': (0.0, 0.1)}
    factors = {'L0_gnn_attn_b': 174.29}
    for name, (base, spread) in spreads.items():
        noise = np.random.default_rng([zlib.crc32(name.encode()), seed]).standard_normal(out[name].shape)
        drawn = base * np.exp(spread * noise) if base else spread * noise
        out[name] = jnp.asarray(drawn.astype(out[name].dtype))
    for name, factor in factors.items():
        out[name] = (out[name] * factor).astype(out[name].dtype)
    return out
```

```python
from collections import namedtuple
from contextlib import ExitStack

import concourse.bass as bass
from concourse import mybir

F32 = mybir.dt.float32
F32R = mybir.dt.float32r
I32 = mybir.dt.int32
ALU = mybir.AluOpType
ACT = mybir.ActivationFunctionType
AX_X = mybir.AxisListType.X

P = 128
GG = 4
TOK = GG * P
EPS = 1e-5
SLOPE = 0.2
BIG = 1e30
LOOP_FROM, LOOP_TO = 10, 43
HRING = 6
GRING = 4
HBANKS = 3
HI_ON_ACT = (0, 2, 4, 6)

Item = namedtuple("Item", "l g q before")


def build(nc, x, adj, attn_w, attn_b, W1, b1, W2, b2, g1, beta1, g2, beta2, out):
    G, N, D = x.shape
    L, _, H = W1.shape
    assert N == P and D == 2 * P and G % GG == 0
    NG = G // GG
    KD = D // P
    C = H // P
    LAST = 3 * (NG - 1) + 4 * (L - 1)

    def exists(s):
        return s >= 0 and 0 <= s // L - s % L < NG

    def ordinal(s):
        return sum(exists(t) for t in range(s))

    def item(s):
        if not exists(s):
            return None
        return Item(s % L, s // L - s % L, ordinal(s), ordinal(s - 4) if s % L else None)

    def loop_item(s, k):
        first, second = item(s), item(s + L)
        assert second.g == first.g + 1 and second.q == first.q + L
        linear = s % L and second.before == first.before + L
        before = k * L + first.before if linear else None
        return Item(s % L, k + first.g, k * L + first.q, before)

    def for_all_slots(eng, slot, first):
        for s in range(first, LOOP_FROM):
            slot(s, lambda d: item(s + d))
        with eng.Fori(0, (LOOP_TO - LOOP_FROM) // L) as k:
            for s in range(LOOP_FROM, LOOP_FROM + L):
                slot(s, lambda d: loop_item(s + d, k))
        for s in range(LOOP_TO, LAST + 2):
            slot(s, lambda d: item(s + d))

    def wait(eng, sem, n):
        if not isinstance(n, int) or n > 0:
            eng.wait_ge(sem, n)

    with ExitStack() as ctx:
        def sb(name, shape, dt=F32):
            return ctx.enter_context(nc.sbuf_tensor(name, shape, dt))

        def sem(name):
            return ctx.enter_context(nc.semaphore(name))

        w1hi = sb("w1hi", [P, L, KD, H], F32R)
        w1lo = sb("w1lo", [P, L, KD, H], F32R)
        w2hi = sb("w2hi", [P, L, C, D], F32R)
        w2lo = sb("w2lo", [P, L, C, D], F32R)
        hid_hi = sb("hid_hi", [P, HRING, TOK], F32R)
        hid_lo = sb("hid_lo", [P, HRING, TOK], F32R)
        gel = sb("gel", [P, GRING, TOK])
        ht32 = sb("ht32", [P, L, KD, TOK])
        ht_hi = sb("ht_hi", [P, KD, TOK], F32R)
        ht_lo = sb("ht_lo", [P, KD, TOK], F32R)
        xs = sb("xs", [P, L, GG, D])
        y2t = sb("y2t", [P, KD, TOK])
        stage = sb("stage", [P, 2, H])
        xres = stage[:, 0, :].rearrange("p (g d) -> p g d", g=GG)
        xout = stage[:, 1, :].rearrange("p (g d) -> p g d", g=GG)
        xraw = sb("xraw", [P, GG, D])
        adji = sb("adji", [P, L, GG, P], I32)
        scores = sb("scores", [P, 2, GG * P])
        pen = scores[:, 0].rearrange("p (g j) -> p g j", g=GG)
        sc = scores[:, 1].rearrange("p (g j) -> p g j", g=GG)
        junk = scores[:].rearrange("p a b -> p (a b)").bitcast(mybir.dt.bfloat16).rearrange(
            "p (n d) -> p n d", d=D)
        E = sb("E", [P, GG, P])
        ET = sb("ET", [P, GG, P])
        ident = sb("ident", [P, P])
        diag = sb("diag", [P, P])
        fence = sb("fence", [P, 1])
        attn_rows = sb("attn_rows", [P, L, 2, D])
        ln2_rows = sb("ln2_rows", [P, 2, L, D])
        attn_bias = sb("attn_bias", [P, L])
        NV = L * (C + 3 * KD)
        vec_rows = sb("vec_rows", [NV, P])
        vec = sb("vec", [P, NV])
        dots = sb("dots", [P, 2, GG])
        si = sb("si", [P, GG])
        mx = sb("mx", [P, GG])
        zm = sb("zm", [P, GG])
        mrow = sb("mrow", [P, GG])
        negm = sb("negm", [P, GG])
        den = sb("den", [P, GG])
        rden = sb("rden", [P, GG])
        halfs = sb("halfs", [P, GG])
        st = {n: sb(f"st{n}", [P, GG, 6]) for n in "012"}
        mv = {n: sb(f"mv{n}", [P, GG, 2]) for n in "012"}
        ve = {n: sb(f"ve{n}", [P, GG]) for n in "012"}
        rstd = {n: sb(f"rstd{n}", [P, GG]) for n in "012"}
        nmr = {n: sb(f"nmr{n}", [P, GG]) for n in "02"}

        def b1c(l, c): return vec[:, l * C + c:l * C + c + 1]
        def dcol(n, l, m):
            at = L * C + (n * L + l) * KD + m
            return vec[:, at:at + 1]
        def b2c(l, m): return dcol(0, l, m)
        def g1c(l, m): return dcol(1, l, m)
        def beta1c(l, m): return dcol(2, l, m)

        hbank = [ctx.enter_context(nc.psum_tensor(f"hbank{i}", [P, TOK], F32)) for i in range(HBANKS)]
        acc = [ctx.enter_context(nc.psum_tensor(f"acc{i}", [P, TOK], F32)) for i in range(KD)]
        turn = [ctx.enter_context(nc.psum_tensor(f"turn{i}", [P, TOK], F32)) for i in range(2)]
        sbank = ctx.enter_context(nc.psum_tensor("sbank", [P, TOK], F32))

        const_in = sem("const_in")
        const_set = sem("const_set")
        vec_turned = sem("vec_turned")
        vec_ready = sem("vec_ready")
        w_in = [sem(f"w_in{i}") for i in range(2)]
        w_hi = sem("w_hi")
        w_lo = sem("w_lo")
        adj_in = [sem(f"adj_in{l}") for l in range(L)]
        xraw_in = sem("xraw_in")
        xres_in = sem("xres_in")
        out_in_dram = sem("out_in_dram")
        ffn1_n = sem("ffn1_n")
        ffn2_n = sem("ffn2_n")
        agg_n = sem("agg_n")
        ytok_n = sem("ytok_n")
        sjb_n = sem("sjb_n")
        et_n = sem("et_n")
        zt_n = sem("zt_n")
        y2t_n = sem("y2t_n")
        pen_n = sem("pen_n")
        dots_n = sem("dots_n")
        si_n = sem("si_n")
        mask_n = sem("mask_n")
        mx_n = sem("mx_n")
        zm_n = sem("zm_n")
        mrow_n = sem("mrow_n")
        negm_n = sem("negm_n")
        z_n = sem("z_n")
        score_n = sem("score_n")
        rden_n = sem("rden_n")
        y1_n = sem("y1_n")
        z1_n = sem("z1_n")
        htlo_n = sem("htlo_n")
        hthi_v = sem("hthi_v")
        st_n = {n: sem(f"st{n}_n") for n in "012"}
        mv_n = {n: sem(f"mv{n}_n") for n in "012"}
        ve_n = {n: sem(f"ve{n}_n") for n in "012"}
        nmr_n = {n: sem(f"nmr{n}_n") for n in "02"}
        hi_v = sem("hi_v")
        lo_n = sem("lo_n")
        gelu_n = sem("gelu_n")
        hi_a = sem("hi_a")
        z2_n = sem("z2_n")
        ht32_n = sem("ht32_n")
        hthi_n = sem("hthi_n")
        exp_n = sem("exp_n")
        et_sb = sem("et_sb")
        x0_n = sem("x0_n")
        rstd_n = {n: sem(f"rstd{n}_n") for n in "012"}
        gam_n = sem("gam_n")
        x_n = sem("x_n")
        out_ready = sem("out_ready")

        block = ctx.enter_context(nc.Block())

        def group(t, g):
            return t.rearrange("(n g) p d -> n p g d", g=GG)[g]

        halves = [(l, w, h) for l in range(L) for w in range(2) for h in range(2)]

        def half_in_dram(l, w, h):
            if w == 0:
                return W1[l, h * P:(h + 1) * P, :]
            return W2[l].rearrange("(h c p) d -> h p c d", h=2, p=P)[h]

        def half_on_chip(parts, l, w, h):
            t = parts[w]
            return t[:, l, h, :] if w == 0 else t[:, l, h * (C // 2):(h + 1) * (C // 2), :]

        def half_staged(n, w):
            t = stage[:, n % 2, :]
            return t if w == 0 else t.rearrange("p (c d) -> p c d", d=D)

        @block.sync
        def _(sp):
            rows = 0
            for t, pieces in ((b1, C), (b2, KD), (g1, KD), (beta1, KD)):
                n = L * pieces
                sp.dma_start(vec_rows[rows:rows + n, :], t.rearrange("l (c p) -> (l c) p", p=P)).then_inc(const_in, 16)
                rows += n
            sp.dma_start(attn_rows[:], attn_w.rearrange("l (t d) -> l t d", t=2).partition_broadcast(P)).then_inc(const_in, 16)
            sp.dma_start(ln2_rows[:, 0], g2.partition_broadcast(P)).then_inc(const_in, 16)
            sp.dma_start(ln2_rows[:, 1], beta2.partition_broadcast(P)).then_inc(const_in, 16)
            sp.dma_start(attn_bias[:], attn_b.partition_broadcast(P)).then_inc(const_in, 16)

            def load_xraw(i, done):
                wait(sp, x0_n, done)
                sp.dma_start(xraw[:], group(x, i.g)).then_inc(xraw_in, 16)

            def load_adj(i, done):
                wait(sp, pen_n, done)
                sp.dma_start(adji[:, i.l], group(adj, i.g)).then_inc(adj_in[i.l], 16)

            def load_weights(n):
                l, w, h = halves[n]
                wait(sp, w_lo, n - 1)
                sp.dma_start(half_staged(n, w), half_in_dram(l, w, h)).then_inc(w_in[n % 2], 16)

            load_xraw(item(0), 0)
            for s in (0, 4, 8):
                if exists(s):
                    load_adj(item(s), 0)
            for n in range(4):
                load_weights(n)
            load_xraw(item(3), GG)

            def slot(s, at):
                if s % L == 1 and at(5):
                    load_xraw(at(5), GG * at(5).g)
                if s % L == 1 and at(1):
                    wait(sp, out_ready, at(1).g)
                    sp.dma_start(xres, group(x, at(1).g)).then_inc(xres_in, 16)
                if at(4) and at(1):
                    load_adj(at(4), at(1).q + 1 if at(1) else 0)
                if s in (1, 2):
                    for n in range(4 * s, 4 * s + 4):
                        load_weights(n)
                if s == 6:
                    sp.wait_ge(w_lo, len(halves))
                if s % L == 0 and at(-1):
                    wait(sp, out_ready, at(-1).g + 1)
                    sp.dma_start(group(out, at(-1).g), xout).then_inc(out_in_dram, 16)

            for_all_slots(sp, slot, -1)
            sp.wait_ge(out_in_dram, 16 * NG)

        @block.gpsimd
        def _(pool):
            pool.memset(ident[:], 0.0).then_inc(const_set, 1)
            pool.memset(diag[:], -BIG).then_inc(const_set, 1)
            pool.memset(halfs[:], -0.5).then_inc(const_set, 1)
            pool.wait_ge(const_set, 3)
            for t, fill in ((ident, 1.0), (diag, BIG)):
                pool.affine_select(out=t[:], in_=t[:], compare_op=ALU.not_equal, fill=fill, base=0,
                                   pattern=[[-1, P]], channel_multiplier=1).then_inc(const_set, 1)
            pool.wait_ge(const_set, 5)
            pool.wait_ge(const_in, 16 * 8)

            def make_rstd(n, q):
                pool.wait_ge(ve_n[n], q + 1)
                pool.tensor_tensor(rstd[n][:], ve[n][:], halfs[:], ALU.pow).then_inc(rstd_n[n], 1)

            def next_x(i):
                t = xs[:, i.l + 1] if i.l < L - 1 else xout
                pool.wait_ge(z2_n, GG * (i.q + 1))
                pool.tensor_tensor(t, t, ln2_rows[:, 0, i.l].unsqueeze(1).to_broadcast([P, GG, D]),
                                   ALU.mult).then_inc(gam_n, 1)
                pool.wait_ge(gam_n, i.q + 1)
                pool.tensor_tensor(t, t, ln2_rows[:, 1, i.l].unsqueeze(1).to_broadcast([P, GG, D]),
                                   ALU.add).then_inc(x_n, 1)
                if i.l == L - 1:
                    pool.wait_ge(x_n, i.q + 1)
                    pool.wait_ge(xres_in, 16 * (i.g + 1))
                    pool.tensor_tensor(t, t, xres, ALU.add).then_inc(out_ready, 1)

            def slot(s, at):
                if at(1):
                    wait(pool, z1_n, GG * at(1).q)
                    make_rstd("1", at(1).q)
                if at(-1):
                    wait(pool, z2_n, GG * at(-1).q)
                    make_rstd("2", at(-1).q)
                    next_x(at(-1))
                if s % L == 0 and at(3):
                    wait(pool, x0_n, GG * at(3).g)
                    make_rstd("0", at(3).g)

            for_all_slots(pool, slot, -3)

        @block.vector
        def _(dve):
            dve.wait_ge(const_in, 16 * 8)
            dve.wait_ge(vec_turned, 1)
            dve.tensor_copy(vec[:], sbank[:, 0:NV]).then_inc(vec_ready, 1)
            dve.wait_ge(vec_ready, 1)

            def split_weights(l):
                for n in range(4 * l, 4 * l + 4):
                    dve.wait_ge(w_hi, n + 1)
                    dve.tensor_tensor(half_on_chip((w1lo, w2lo), *halves[n]), half_staged(n, halves[n][1]),
                                      half_on_chip((w1hi, w2hi), *halves[n]).bitcast(F32),
                                      ALU.subtract).then_inc(w_lo, 1)

            def stats(n, q, src, ready=None, per=1):
                for g in range(GG):
                    if ready and g % per == 0:
                        dve.wait_ge(ready, (GG // per) * q + g // per + 1)
                    dve.bn_stats(st[n][:, g], src(g)).then_inc(st_n[n], 1)
                dve.wait_ge(st_n[n], GG * (q + 1))
                dve.memset(fence[:], 0.0)
                for g in range(GG):
                    dve.bn_aggr(mv[n][:, g], st[n][:, g]).then_inc(mv_n[n], 1)
                dve.wait_ge(mv_n[n], GG * (q + 1))
                dve.tensor_scalar(ve[n][:], mv[n][:, :, 1], EPS, None, ALU.add).then_inc(ve_n[n], 1)

            def minus_mean(n, q):
                dve.wait_ge(rstd_n[n], q + 1)
                dve.scalar_tensor_tensor(out=nmr[n][:], in0=mv[n][:, :, 0], scalar=-1.0, in1=rstd[n][:],
                                         op0=ALU.mult, op1=ALU.mult).then_inc(nmr_n[n], 1)

            def split(i, c):
                hi, lo, g32 = hid_hi[:, c % HRING], hid_lo[:, c % HRING], gel[:, c % GRING]
                if c >= HRING:
                    dve.wait_ge(ffn2_n, C * i.q + c - HRING + 1)
                if c in HI_ON_ACT:
                    dve.wait_ge(hi_a, len(HI_ON_ACT) * i.q + HI_ON_ACT.index(c) + 1)
                else:
                    dve.wait_ge(gelu_n, C * i.q + c + 1)
                    if c < HRING:
                        wait(dve, ffn2_n, C * i.q)
                    mine = [n for n in range(C) if n not in HI_ON_ACT]
                    dve.tensor_copy(hi, g32).then_inc(hi_v, 1)
                    dve.wait_ge(hi_v, len(mine) * i.q + mine.index(c) + 1)
                dve.tensor_tensor(lo, g32, hi.bitcast(F32), ALU.subtract).then_inc(lo_n, 1)

            def residual(i):
                wait(dve, ytok_n, 2 * i.q)
                dve.wait_ge(ffn2_n, C * (i.q + 1))
                for m in range(KD):
                    dve.scalar_tensor_tensor(out=y2t[:, m], in0=acc[m][:], scalar=b2c(i.l, m),
                                             in1=ht32[:, i.l, m], op0=ALU.add, op1=ALU.add).then_inc(y2t_n, 1)

            def node_dots(i):
                if i.l == 0:
                    dve.wait_ge(x0_n, GG * (i.g + 1))
                else:
                    dve.wait_ge(x_n, i.before + 1)
                wait(dve, sjb_n, i.q)
                wait(dve, exp_n, GG * i.q)
                for t in (1, 0):
                    for g in range(GG):
                        last = dve.tensor_tensor_reduce(junk[:, GG * t + g], xs[:, i.l, g], attn_rows[:, i.l, t], 1.0, 0.0,
                                                        ALU.mult, ALU.add, dots[:, t, g:g + 1])
                last.then_inc(dots_n, 1)

            def add_bias(i):
                dve.wait_ge(dots_n, i.q + 1)
                dve.tensor_scalar(si[:], dots[:, 0], attn_bias[:, i.l:i.l + 1], None, ALU.add).then_inc(si_n, 1)

            def penalty(i):
                dve.wait_ge(adj_in[i.l], 16 * (i.g + 1))
                dve.wait_ge(dots_n, i.q + 1)
                dve.scalar_tensor_tensor(out=pen[:], in0=adji[:, i.l], scalar=2 * BIG,
                                         in1=diag[:].unsqueeze(1).to_broadcast([P, GG, P]),
                                         op0=ALU.mult, op1=ALU.add).then_inc(pen_n, 1)

            def masked(i):
                dve.wait_ge(pen_n, i.q + 1)
                dve.wait_ge(sjb_n, i.q + 1)
                dve.tensor_tensor(sc[:], pen[:], sbank[:].rearrange("p (g j) -> p g j", g=GG),
                                  ALU.min).then_inc(mask_n, 1)
                dve.wait_ge(mask_n, i.q + 1)
                dve.tensor_reduce(mx[:], sc[:], AX_X, ALU.max).then_inc(mx_n, 1)
                dve.wait_ge(si_n, i.q + 1)
                dve.wait_ge(mx_n, i.q + 1)
                dve.tensor_tensor(sc[:], sc[:], si[:].unsqueeze(2).to_broadcast([P, GG, P]),
                                  ALU.add).then_inc(z_n, 1)
                dve.tensor_tensor(zm[:], mx[:], si[:], ALU.add).then_inc(zm_n, 1)

            def leaky(i):
                dve.wait_ge(z_n, i.q + 1)
                dve.scalar_tensor_tensor(out=sc[:], in0=sc[:], scalar=SLOPE, in1=sc[:],
                                         op0=ALU.mult, op1=ALU.max).then_inc(score_n, 1)
                dve.wait_ge(zm_n, i.q + 1)
                dve.scalar_tensor_tensor(out=mrow[:], in0=zm[:], scalar=SLOPE, in1=zm[:],
                                         op0=ALU.mult, op1=ALU.max).then_inc(mrow_n, 1)
                dve.wait_ge(mrow_n, i.q + 1)
                dve.tensor_scalar(negm[:], mrow[:], -1.0, None, ALU.mult).then_inc(negm_n, 1)

            def attend(i):
                dve.wait_ge(exp_n, GG * (i.q + 1))
                dve.reciprocal(rden[:], den[:]).then_inc(rden_n, 1)
                dve.wait_ge(rden_n, i.q + 1)
                for g in range(GG):
                    if g % 2 == 0:
                        dve.wait_ge(agg_n, 2 * i.q + g // 2 + 1)
                    dve.scalar_tensor_tensor(out=xs[:, i.l, g], in0=acc[g // 2][:, (g % 2) * D:(g % 2 + 1) * D],
                                             scalar=rden[:, g:g + 1], in1=xs[:, i.l, g],
                                             op0=ALU.mult, op1=ALU.add).then_inc(y1_n, 1)

            def norm1(i):
                dve.wait_ge(rstd_n["1"], i.q + 1)
                for g in range(GG):
                    dve.tensor_scalar(xs[:, i.l, g], xs[:, i.l, g], mv["1"][:, g, 0:1], rstd["1"][:, g:g + 1],
                                      ALU.subtract, ALU.mult).then_inc(z1_n, 1)

            def h_low(i, f):
                for m in range(KD):
                    dve.wait_ge(hthi_n, KD * i.q + m + 1)
                    if f and m == 0:
                        dve.wait_ge(ffn1_n, C * (f.q + 1))
                    dve.tensor_tensor(ht_lo[:, m], ht32[:, i.l, m], ht_hi[:, m].bitcast(F32),
                                      ALU.subtract).then_inc(htlo_n, 1)

            def slot(s, at):
                f, t, b, a = at(0), at(-1), at(1), at(2)
                p = at(3) if s % L == 0 else None
                if t: residual(t)
                if a:
                    node_dots(a)
                    penalty(a)
                if f: split(f, 0)
                if b:
                    attend(b)
                    stats("1", b.q, lambda g: xs[:, b.l, g], y1_n, 1)
                if f: split(f, 1)
                if t:
                    stats("2", t.q, lambda g: turn[g // 2][:, (g % 2) * D:(g % 2 + 1) * D], ytok_n, 2)
                if a: add_bias(a)
                if f: split(f, 2)
                if b: norm1(b)
                if t: minus_mean("2", t.q)
                if f: split(f, 3)
                if a: masked(a)
                if f: split(f, 4)
                if a: leaky(a)
                if f: split(f, 5)
                if p:
                    dve.wait_ge(xraw_in, 16 * (p.g + 1))
                    stats("0", p.g, lambda g: xraw[:, g])
                if b: h_low(b, f)
                if f: split(f, 6)
                if p: minus_mean("0", p.g)
                if f: split(f, 7)
                if s in (-1, 1, 2):
                    split_weights(max(s, 0))

            for_all_slots(dve, slot, -3)

        @block.scalar
        def _(act):
            act.wait_ge(vec_ready, 1)

            def round_weights(l):
                for n in range(4 * l, 4 * l + 4):
                    act.wait_ge(w_in[n % 2], 16 * (n // 2 + 1))
                    act.copy(half_on_chip((w1hi, w2hi), *halves[n]), half_staged(n, halves[n][1])).then_inc(w_hi, 1)

            def gelu(i, c):
                act.wait_ge(ffn1_n, C * i.q + c + 1)
                wait(act, lo_n, C * i.q + c - GRING + 1)
                act.activation(gel[:, c % GRING], hbank[c % HBANKS][:], ACT.Gelu, bias=b1c(i.l, c)).then_inc(gelu_n, 1)

            def high(i, c):
                if c not in HI_ON_ACT:
                    return
                act.wait_ge(gelu_n, C * i.q + c + 1)
                if c < HRING:
                    wait(act, ffn2_n, C * i.q)
                else:
                    act.wait_ge(ffn2_n, C * i.q + c - HRING + 1)
                act.copy(hid_hi[:, c % HRING], gel[:, c % GRING]).then_inc(hi_a, 1)

            def norm2(i, f):
                t = xs[:, i.l + 1] if i.l < L - 1 else xout
                act.wait_ge(nmr_n["2"], i.q + 1)
                if f and i.l < L - 1:
                    act.wait_ge(zt_n, KD * (f.q + 1))
                if i.l == L - 1:
                    wait(act, out_in_dram, 16 * i.g)
                for g in range(GG):
                    act.activation(t[:, g], turn[g // 2][:, (g % 2) * D:(g % 2 + 1) * D], ACT.Identity,
                                   bias=nmr["2"][:, g:g + 1], scale=rstd["2"][:, g:g + 1]).then_inc(z2_n, 1)

            def h_high(i, f):
                for m in range(KD):
                    act.wait_ge(zt_n, KD * i.q + m + 1)
                    act.activation(ht32[:, i.l, m], turn[m][:], ACT.Identity, bias=beta1c(i.l, m),
                                   scale=g1c(i.l, m)).then_inc(ht32_n, 1)
                for m in range(KD):
                    act.wait_ge(ht32_n, KD * i.q + m + 1)
                    if f and m == 0:
                        act.wait_ge(ffn1_n, C * (f.q + 1))
                    act.copy(ht_hi[:, m], ht32[:, i.l, m]).then_inc(hthi_n, 1)

            def exps(i):
                act.wait_ge(score_n, i.q + 1)
                act.wait_ge(negm_n, i.q + 1)
                wait(act, et_n, i.q)
                wait(act, rden_n, i.q)
                for g in range(GG):
                    act.activation(E[:, g], sc[:, g], ACT.Exp, bias=negm[:, g:g + 1],
                                   accum_out=den[:, g:g + 1]).then_inc(exp_n, 1)

            def et_out(i):
                act.wait_ge(et_n, i.q + 1)
                wait(act, agg_n, 2 * i.q)
                act.copy(ET[:].rearrange("p g j -> p (g j)"), sbank[:]).then_inc(et_sb, 1)

            def first_x(i, f):
                act.wait_ge(nmr_n["0"], i.g + 1)
                if f:
                    act.wait_ge(zt_n, KD * (f.q + 1))
                for g in range(GG):
                    act.activation(xs[:, 0, g], xraw[:, g], ACT.Relu, bias=nmr["0"][:, g:g + 1],
                                   scale=rstd["0"][:, g:g + 1]).then_inc(x0_n, 1)

            def slot(s, at):
                f, t, b, a = at(0), at(-1), at(1), at(2)
                p = at(3) if s % L == 0 else None
                if f:
                    for c in range(6):
                        gelu(f, c)
                        if c: high(f, c - 1)
                if t: norm2(t, f)
                if f:
                    gelu(f, 6)
                    high(f, 5)
                    gelu(f, 7)
                if b: h_high(b, f)
                if f: high(f, 6)
                if a: exps(a)
                if f: high(f, 7)
                if a: et_out(a)
                if p: first_x(p, f)
                if s in (-1, 1, 2):
                    round_weights(max(s, 0))

            for_all_slots(act, slot, -3)

        @block.tensor
        def _(pe):
            pe.wait_ge(const_in, 16 * 8)
            pe.wait_ge(const_set, 5)
            pe.transpose(sbank[:, 0:NV], vec_rows[:], ident[0:NV, 0:NV]).then_inc(vec_turned, 1)
            pe.wait_ge(vec_ready, 1)

            def ffn1(i, c):
                if c == 0:
                    pe.wait_ge(htlo_n, KD * (i.q + 1))
                wait(pe, gelu_n, C * i.q + max(c - HBANKS + 1, 0))
                at_c = slice(c * P, (c + 1) * P)
                for k in range(KD):
                    for n, (w, v) in enumerate(((w1hi, ht_hi), (w1hi, ht_lo), (w1lo, ht_hi))):
                        mm = pe.matmul(hbank[c % HBANKS][:], w[:, i.l, k, at_c], v[:, k],
                                       start=k == 0 and n == 0, stop=k == KD - 1 and n == 2)
                mm.then_inc(ffn1_n, 1)

            def ffn2(i, c):
                pe.wait_ge(lo_n, C * i.q + c + 1)
                for n, (w, v) in enumerate(((w2hi, hid_hi), (w2hi, hid_lo), (w2lo, hid_hi))):
                    for m in range(KD):
                        mm = pe.matmul(acc[m][:], w[:, i.l, c, m * P:(m + 1) * P], v[:, c % HRING],
                                       start=c == 0 and n == 0, stop=c == C - 1 and n == 2)
                mm.then_inc(ffn2_n, 1)

            def aggregate(i, t):
                if t:
                    pe.wait_ge(y2t_n, KD * (t.q + 1))
                pe.wait_ge(et_sb, i.q + 1)
                for g in range(GG):
                    mm = pe.matmul(acc[g // 2][:, (g % 2) * D:(g % 2 + 1) * D], ET[:, g], xs[:, i.l, g],
                                   start=True, stop=True)
                    if g % 2:
                        mm.then_inc(agg_n, 1)

            def y2_back(i):
                pe.wait_ge(y2t_n, KD * (i.q + 1))
                for g in range(GG):
                    for m in range(KD):
                        mm = pe.transpose(turn[g // 2][:, (g % 2) * D + m * P:(g % 2) * D + (m + 1) * P],
                                          y2t[:, m, g * P:(g + 1) * P], ident[:])
                    if g % 2:
                        mm.then_inc(ytok_n, 1)

            def sj_rows(i):
                pe.wait_ge(dots_n, i.q + 1)
                wait(pe, et_sb, i.q)
                for g in range(GG):
                    mm = pe.transpose(sbank[:, g * P:(g + 1) * P], dots[:, 1, g:g + 1].to_broadcast([P, P]), ident[:])
                mm.then_inc(sjb_n, 1)

            def z1_turn(i, t):
                pe.wait_ge(z1_n, GG * (i.q + 1))
                if t:
                    pe.wait_ge(z2_n, GG * (t.q + 1))
                for m in range(KD):
                    for g in range(GG):
                        mm = pe.transpose(turn[m][:, g * P:(g + 1) * P], xs[:, i.l, g, m * P:(m + 1) * P], ident[:])
                    mm.then_inc(zt_n, 1)

            def e_turn(i):
                pe.wait_ge(exp_n, GG * (i.q + 1))
                for g in range(GG):
                    mm = pe.transpose(sbank[:, g * P:(g + 1) * P], E[:, g], ident[:])
                mm.then_inc(et_n, 1)

            def slot(s, at):
                f, t, b, a = at(0), at(-1), at(1), at(2)
                if s == 0:
                    pe.wait_ge(w_lo, 4)
                if s == 4:
                    pe.wait_ge(w_lo, 4 * L)
                if f: ffn1(f, 0)
                if t: y2_back(t)
                if f: ffn1(f, 1)
                if b: aggregate(b, t)
                if f:
                    ffn1(f, 2)
                    ffn1(f, 3)
                if a: sj_rows(a)
                if f:
                    for c in range(4, 8):
                        ffn1(f, c)
                if b: z1_turn(b, t)
                if f:
                    if b:
                        pe.wait_ge(y1_n, GG * (b.q + 1))
                    elif t:
                        pe.wait_ge(y2t_n, KD * (t.q + 1))
                    for c in range(4):
                        ffn2(f, c)
                if a: e_turn(a)
                if f:
                    for c in range(4, 8):
                        ffn2(f, c)

            for_all_slots(pe, slot, -3)


_INS = ["x", "adj"] + ["L0_gnn_" + n for n in
                       ("attn_w", "attn_b", "W1", "b1", "W2", "b2", "g1", "beta1", "g2", "beta2")]


def kernel(**inputs):
    import numpy as np
    import concourse.bacc as bacc
    from concourse.bass_utils import run_bass_kernel_spmd as run

    nc = bacc.Bacc("TRN2", target_bir_lowering=False, num_devices=1)
    arrays, args = {}, []
    for name in _INS:
        a = np.ascontiguousarray(inputs[name])
        arrays[f"in_{name}_dram"] = a
        args.append(nc.dram_tensor(f"in_{name}_dram", a.shape, mybir.dt.from_np(a.dtype), kind="ExternalInput").ap())
    shape = arrays["in_x_dram"].shape
    args.append(nc.dram_tensor("out_dram", shape, F32, kind="ExternalOutput").ap())
    build(nc, *args)
    return run(nc, [arrays], core_ids=[0]).results[0]["out_dram"]
```

```python
from collections import namedtuple
from contextlib import ExitStack

import concourse.bass as bass
from concourse import mybir

F32 = mybir.dt.float32
F32R = mybir.dt.float32r
I32 = mybir.dt.int32
ALU = mybir.AluOpType
ACT = mybir.ActivationFunctionType
AX_X = mybir.AxisListType.X

P = 128
GG = 4
TOK = GG * P
EPS = 1e-5
SLOPE = 0.2
BIG = 1e30
BATCH = 4
LOOP_FROM, LOOP_TO = 8, 44
RING = 3
HRING = 6
GRING = 4
HBANKS = 3

Item = namedtuple("Item", "q l g r nth")


def build(nc, x, adj, attn_w, attn_b, W1, b1, W2, b2, g1, beta1, g2, beta2, out):
    G, N, D = x.shape
    L, _, H = W1.shape
    assert N == P and D == 2 * P and G % GG == 0
    NG = G // GG
    KD = D // P
    C = H // P
    ROUND = BATCH * L
    ITEMS = NG * L
    EARLY = GRING // 2
    assert NG % BATCH == 0 and ROUND % RING == 0 and LOOP_TO + 4 <= ITEMS
    assert (LOOP_TO - LOOP_FROM) % ROUND == 0

    def item(s, k=0):
        if not 0 <= s < ITEMS:
            return None
        return Item(k * ROUND + s, s % ROUND // BATCH, k * BATCH + (s // ROUND * BATCH + s % BATCH),
                    s % RING, k * (ROUND // RING) + s // RING)

    def is_item(i, first, last):
        return isinstance(i.q, int) and first <= i.q <= last

    def for_all_slots(eng, slot, first):
        for s in range(first, LOOP_FROM):
            slot(s, lambda d: item(s + d))
        with eng.Fori(0, (LOOP_TO - LOOP_FROM) // ROUND) as k:
            for s in range(LOOP_FROM, LOOP_FROM + ROUND):
                slot(s, lambda d: item(s + d, k))
        for s in range(LOOP_TO, ITEMS + 1):
            slot(s, lambda d: item(s + d))

    def wait(eng, sem, n):
        if not isinstance(n, int) or n > 0:
            eng.wait_ge(sem, n)

    with ExitStack() as ctx:
        def sb(name, shape, dt=F32):
            return ctx.enter_context(nc.sbuf_tensor(name, shape, dt))

        def sem(name):
            return ctx.enter_context(nc.semaphore(name))

        w1hi = sb("w1hi", [P, L, KD, H], F32R)
        w1lo = sb("w1lo", [P, L, KD, H], F32R)
        w2hi = sb("w2hi", [P, L, C, D], F32R)
        w2lo = sb("w2lo", [P, L, C, D], F32R)
        hid_hi = sb("hid_hi", [P, HRING, TOK], F32R)
        hid_lo = sb("hid_lo", [P, HRING, TOK], F32R)
        gel = sb("gel", [P, GRING, TOK])
        ht32 = sb("ht32", [P, RING, KD, TOK])
        ht_hi = sb("ht_hi", [P, KD, TOK], F32R)
        ht_lo = sb("ht_lo", [P, KD, TOK], F32R)
        xs = sb("xs", [P, RING, GG, D])
        y2t = sb("y2t", [P, KD, TOK])
        stage = sb("stage", [P, 2, H])
        xres = stage[:, 0, :].rearrange("p (g d) -> p g d", g=GG)
        xout = stage[:, 1, :].rearrange("p (g d) -> p g d", g=GG)
        xraw = sb("xraw", [P, GG, D])
        early = [gel[:, 2 * i:2 * i + 2].rearrange("p a (g d) -> p (a g) d", d=D)
                 for i in range(EARLY)]
        adji = sb("adji", [P, RING, GG, P], I32)
        scores = sb("scores", [P, 2, GG * P])
        pen = scores[:, 0].rearrange("p (g j) -> p g j", g=GG)
        sc = scores[:, 1].rearrange("p (g j) -> p g j", g=GG)
        junk = scores[:].rearrange("p a b -> p (a b)").bitcast(mybir.dt.bfloat16).rearrange(
            "p (n d) -> p n d", d=D)
        E = sb("E", [P, GG, P])
        ET = sb("ET", [P, GG, P])
        ident = sb("ident", [P, P])
        diag = sb("diag", [P, P])
        warm = sb("warm", [P, 2])
        fence = sb("fence", [P, 1])
        pool_fence = sb("pool_fence", [P, 1])
        attn_rows = sb("attn_rows", [P, L, 2, D])
        ln2_rows = sb("ln2_rows", [P, 2, L, D])
        attn_bias = sb("attn_bias", [P, L])
        NV = L * (C + 3 * KD)
        vec_rows = sb("vec_rows", [NV, P])
        vec = sb("vec", [P, NV])
        dots = sb("dots", [P, 2, GG])
        si = sb("si", [P, GG])
        mx = sb("mx", [P, GG])
        zm = sb("zm", [P, GG])
        mrow = sb("mrow", [P, GG])
        negm = sb("negm", [P, GG])
        den = sb("den", [P, GG])
        rden = sb("rden", [P, GG])
        halfs = sb("halfs", [P, GG])
        st = {n: sb(f"st{n}", [P, GG, 6]) for n in "012"}
        mv = {n: sb(f"mv{n}", [P, GG, 2]) for n in "012"}
        ve = {n: sb(f"ve{n}", [P, GG]) for n in "012"}
        rstd = {n: sb(f"rstd{n}", [P, GG]) for n in "012"}
        nmr = {n: sb(f"nmr{n}", [P, GG]) for n in "02"}

        def b1c(l, c): return vec[:, l * C + c:l * C + c + 1]
        def dcol(n, l, m):
            at = L * C + (n * L + l) * KD + m
            return vec[:, at:at + 1]
        def b2c(l, m): return dcol(0, l, m)
        def g1c(l, m): return dcol(1, l, m)
        def beta1c(l, m): return dcol(2, l, m)

        hbank = [ctx.enter_context(nc.psum_tensor(f"hbank{i}", [P, TOK], F32)) for i in range(HBANKS)]
        zbank = (hbank[2], hbank[0])
        acc = [ctx.enter_context(nc.psum_tensor(f"acc{i}", [P, TOK], F32)) for i in range(KD)]
        turn = [ctx.enter_context(nc.psum_tensor(f"turn{i}", [P, TOK], F32)) for i in range(2)]
        sbank = ctx.enter_context(nc.psum_tensor("sbank", [P, TOK], F32))

        vec_in = sem("vec_in")
        attn_in = sem("attn_in")
        ln2_in = sem("ln2_in")
        const_set = sem("const_set")
        vec_turned = sem("vec_turned")
        vec_ready = sem("vec_ready")
        w_in = [sem(f"w_in{i}") for i in range(2)]
        w_hi = sem("w_hi")
        w_lo = sem("w_lo")
        adj_in = [sem(f"adj_in{r}") for r in range(RING)]
        early_in = [sem(f"early_in{i}") for i in range(EARLY)]
        xraw_in = sem("xraw_in")
        xres_in = sem("xres_in")
        xout_free = sem("xout_free")
        ffn1_n = sem("ffn1_n")
        ffn2_n = sem("ffn2_n")
        agg_n = sem("agg_n")
        ytok_n = sem("ytok_n")
        sjb_n = sem("sjb_n")
        et_n = sem("et_n")
        zt_n = sem("zt_n")
        y2t_n = sem("y2t_n")
        pen_n = sem("pen_n")
        dots_n = sem("dots_n")
        si_n = sem("si_n")
        mask_n = sem("mask_n")
        mx_n = sem("mx_n")
        zm_n = sem("zm_n")
        mrow_n = sem("mrow_n")
        negm_n = sem("negm_n")
        z_n = sem("z_n")
        score_n = sem("score_n")
        rden_n = sem("rden_n")
        y1_n = sem("y1_n")
        z1_n = sem("z1_n")
        htlo_n = sem("htlo_n")
        st_n = {n: sem(f"st{n}_n") for n in "012"}
        mv_n = {n: sem(f"mv{n}_n") for n in "012"}
        ve_n = {n: sem(f"ve{n}_n") for n in "012"}
        nmr_n = {n: sem(f"nmr{n}_n") for n in "02"}
        lo_n = sem("lo_n")
        gelu_n = sem("gelu_n")
        hi_n = sem("hi_n")
        z2_n = sem("z2_n")
        ht32_n = sem("ht32_n")
        hthi_n = sem("hthi_n")
        exp_n = sem("exp_n")
        warm_n = sem("warm_n")
        et_sb = sem("et_sb")
        x0_n = sem("x0_n")
        rstd_n = {n: sem(f"rstd{n}_n") for n in "012"}
        gam_n = sem("gam_n")
        x_n = sem("x_n")
        out_ready = sem("out_ready")

        block = ctx.enter_context(nc.Block())

        def group(t, g):
            return t.rearrange("(n g) p d -> n p g d", g=GG)[g]

        def raw(i):
            if is_item(i, 1, EARLY):
                return early[i.q - 1], early_in[i.q - 1], 16
            return xraw, xraw_in, 16 * (i.g + 1 if is_item(i, 0, 0) else i.g + 1 - EARLY)

        halves = [(l, w, h) for l in range(L) for w in range(2) for h in range(2)]

        def halves_of_slot(s):
            if s in (-3, -1):
                return range(s + 3, s + 5)
            return range(s + 4, s + 5) if 0 <= s < 4 * (L - 1) else ()

        def half_in_dram(l, w, h):
            if w == 0:
                return W1[l, h * P:(h + 1) * P, :]
            return W2[l].rearrange("(h c p) d -> h p c d", h=2, p=P)[h]

        def half_on_chip(parts, l, w, h):
            t = parts[w]
            return t[:, l, h, :] if w == 0 else t[:, l, h * (C // 2):(h + 1) * (C // 2), :]

        def half_staged(n, w):
            t = stage[:, n % 2, :]
            return t if w == 0 else t.rearrange("p (c d) -> p c d", d=D)

        @block.sync
        def _(sp):
            def load_small():
                rows = 0
                for t, pieces in ((b1, C), (b2, KD), (g1, KD), (beta1, KD)):
                    n = L * pieces
                    sp.dma_start(vec_rows[rows:rows + n, :], t.rearrange("l (c p) -> (l c) p", p=P)).then_inc(vec_in, 16)
                    rows += n
                sp.dma_start(attn_rows[:], attn_w.rearrange("l (t d) -> l t d", t=2).partition_broadcast(P)).then_inc(attn_in, 16)
                sp.dma_start(attn_bias[:], attn_b.partition_broadcast(P)).then_inc(attn_in, 16)

            def load_ln2_rows():
                sp.dma_start(ln2_rows[:, 0], g2.partition_broadcast(P)).then_inc(ln2_in, 16)
                sp.dma_start(ln2_rows[:, 1], beta2.partition_broadcast(P)).then_inc(ln2_in, 16)

            def load_xraw(i):
                t, arrived, _ = raw(i)
                if t is xraw:
                    wait(sp, x0_n, GG * (1 if is_item(i, 1 + EARLY, 1 + EARLY) else i.g))
                sp.dma_start(t[:], group(x, i.g)).then_inc(arrived, 16)

            def load_adj(i):
                wait(sp, pen_n, i.q - RING + 1)
                sp.dma_start(adji[:, i.r], group(adj, i.g)).then_inc(adj_in[i.r], 16)

            def load_weights(n):
                l, w, h = halves[n]
                wait(sp, w_lo, n - 1)
                sp.dma_start(half_staged(n, w), half_in_dram(l, w, h)).then_inc(w_in[n % 2], 16)

            def slot(s, at):
                if at(4) and at(4).l == 0:
                    load_xraw(at(4))
                if s == -4:
                    load_small()
                if at(4):
                    load_adj(at(4))
                for n in halves_of_slot(s + 1):
                    load_weights(n)
                if s == -1:
                    load_ln2_rows()
                if at(-1) and at(-1).l == L - 1:
                    wait(sp, out_ready, at(-1).g + 1)
                    sp.dma_start(group(out, at(-1).g), xout).then_inc(xout_free, 16)
                if at(0) and at(0).l == L - 1:
                    sp.dma_start(xres, group(x, at(0).g)).then_inc(xres_in, 16)

            for_all_slots(sp, slot, -4)
            sp.wait_ge(xout_free, 16 * (NG + 1))

        @block.gpsimd
        def _(pool):
            pool.memset(ident[:], 0.0).then_inc(const_set, 1)
            pool.memset(diag[:], -BIG).then_inc(const_set, 1)
            pool.memset(halfs[:], -0.5).then_inc(const_set, 1)
            pool.memset(warm[:], 0.0).then_inc(const_set, 1)
            pool.wait_ge(const_set, 4)
            for t, fill in ((ident, 1.0), (diag, BIG)):
                pool.affine_select(out=t[:], in_=t[:], compare_op=ALU.not_equal, fill=fill, base=0,
                                   pattern=[[-1, P]], channel_multiplier=1).then_inc(const_set, 1)
            pool.wait_ge(const_set, 6)
            def make_rstd(n, q):
                pool.wait_ge(ve_n[n], q + 1)
                pool.tensor_tensor(rstd[n][:], ve[n][:], halfs[:], ALU.pow).then_inc(rstd_n[n], 1)

            def next_x(i):
                t = xs[:, (i.r + 1) % RING] if i.l < L - 1 else xout
                if is_item(i, 0, 0):
                    pool.wait_ge(ln2_in, 16 * 2)
                pool.wait_ge(z2_n, GG * (i.q + 1))
                pool.tensor_tensor(t, t, ln2_rows[:, 0, i.l].unsqueeze(1).to_broadcast([P, GG, D]),
                                   ALU.mult).then_inc(gam_n, 1)
                pool.wait_ge(gam_n, i.q + 1)
                pool.tensor_tensor(t, t, ln2_rows[:, 1, i.l].unsqueeze(1).to_broadcast([P, GG, D]),
                                   ALU.add).then_inc(x_n, 1)
                if i.l == L - 1:
                    pool.wait_ge(x_n, i.q + 1)
                    pool.wait_ge(xres_in, 16 * (i.g + 1))
                    pool.tensor_tensor(t, t, xres, ALU.add).then_inc(out_ready, 1)

            def slot(s, at):
                if at(1):
                    wait(pool, z1_n, GG * at(1).q)
                    make_rstd("1", at(1).q)
                if at(-1):
                    wait(pool, z2_n, GG * at(-1).q)
                    make_rstd("2", at(-1).q)
                    next_x(at(-1))
                if at(4) and at(4).l == 0:
                    wait(pool, x0_n, GG * at(4).g)
                    make_rstd("0", at(4).g)
                if s == 7:
                    pool.wait_ge(w_lo, len(halves))
                    pool.memset(pool_fence[:], 0.0).then_inc(xout_free, 16)

            for_all_slots(pool, slot, -4)

        @block.vector
        def _(dve):
            def split_weights(ns):
                for n in ns:
                    dve.wait_ge(w_hi, n + 1)
                    dve.tensor_tensor(half_on_chip((w1lo, w2lo), *halves[n]), half_staged(n, halves[n][1]),
                                      half_on_chip((w1hi, w2hi), *halves[n]).bitcast(F32),
                                      ALU.subtract).then_inc(w_lo, 1)

            def moments(n, q, src, ready=None, per=1):
                for g in range(GG):
                    if ready and g % per == 0:
                        dve.wait_ge(ready, (GG // per) * q + g // per + 1)
                    dve.bn_stats(st[n][:, g], src(g)).then_inc(st_n[n], 1)

            def variance(n, q):
                dve.wait_ge(st_n[n], GG * (q + 1))
                dve.memset(fence[:], 0.0)
                for g in range(GG):
                    dve.bn_aggr(mv[n][:, g], st[n][:, g]).then_inc(mv_n[n], 1)
                dve.wait_ge(mv_n[n], GG * (q + 1))
                dve.tensor_scalar(ve[n][:], mv[n][:, :, 1], EPS, None, ALU.add).then_inc(ve_n[n], 1)

            def minus_mean(n, q):
                dve.wait_ge(rstd_n[n], q + 1)
                dve.scalar_tensor_tensor(out=nmr[n][:], in0=mv[n][:, :, 0], scalar=-1.0, in1=rstd[n][:],
                                         op0=ALU.mult, op1=ALU.mult).then_inc(nmr_n[n], 1)

            def split(i, c):
                hi, lo, g32 = hid_hi[:, c % HRING], hid_lo[:, c % HRING], gel[:, c % GRING]
                if c >= HRING:
                    dve.wait_ge(ffn2_n, C * i.q + c - HRING + 1)
                dve.wait_ge(hi_n, C * i.q + c + 1)
                dve.tensor_tensor(lo, g32, hi.bitcast(F32), ALU.subtract).then_inc(lo_n, 1)

            def residual(i):
                wait(dve, ytok_n, 2 * i.q)
                dve.wait_ge(ffn2_n, C * (i.q + 1))
                for m in range(KD):
                    dve.scalar_tensor_tensor(out=y2t[:, m], in0=acc[m][:], scalar=b2c(i.l, m),
                                             in1=ht32[:, i.r, m], op0=ALU.add, op1=ALU.add).then_inc(y2t_n, 1)

            def node_dots(i):
                if i.l == 0:
                    dve.wait_ge(x0_n, GG * (i.g + 1))
                else:
                    dve.wait_ge(x_n, i.q - BATCH + 1)
                wait(dve, sjb_n, i.q)
                wait(dve, exp_n, GG * i.q)
                if is_item(i, 0, 0):
                    dve.wait_ge(attn_in, 16 * 2)
                for t in (1, 0):
                    for g in range(GG):
                        last = dve.tensor_tensor_reduce(junk[:, GG * t + g], xs[:, i.r, g], attn_rows[:, i.l, t], 1.0, 0.0,
                                                        ALU.mult, ALU.add, dots[:, t, g:g + 1])
                last.then_inc(dots_n, 1)

            def add_bias(i):
                dve.wait_ge(dots_n, i.q + 1)
                dve.tensor_scalar(si[:], dots[:, 0], attn_bias[:, i.l:i.l + 1], None, ALU.add).then_inc(si_n, 1)

            def penalty(i):
                dve.wait_ge(adj_in[i.r], 16 * (i.nth + 1))
                dve.wait_ge(dots_n, i.q + 1)
                dve.scalar_tensor_tensor(out=pen[:], in0=adji[:, i.r], scalar=2 * BIG,
                                         in1=diag[:].unsqueeze(1).to_broadcast([P, GG, P]),
                                         op0=ALU.mult, op1=ALU.add).then_inc(pen_n, 1)

            def masked(i):
                dve.wait_ge(pen_n, i.q + 1)
                dve.wait_ge(sjb_n, i.q + 1)
                dve.tensor_tensor(sc[:], pen[:], sbank[:].rearrange("p (g j) -> p g j", g=GG),
                                  ALU.min).then_inc(mask_n, 1)

            def row_max(i):
                dve.wait_ge(mask_n, i.q + 1)
                dve.tensor_reduce(mx[:], sc[:], AX_X, ALU.max).then_inc(mx_n, 1)

            def add_si(i):
                dve.wait_ge(si_n, i.q + 1)
                dve.wait_ge(mx_n, i.q + 1)
                dve.tensor_tensor(sc[:], sc[:], si[:].unsqueeze(2).to_broadcast([P, GG, P]),
                                  ALU.add).then_inc(z_n, 1)
                dve.tensor_tensor(zm[:], mx[:], si[:], ALU.add).then_inc(zm_n, 1)

            def leaky(i):
                dve.wait_ge(z_n, i.q + 1)
                dve.scalar_tensor_tensor(out=sc[:], in0=sc[:], scalar=SLOPE, in1=sc[:],
                                         op0=ALU.mult, op1=ALU.max).then_inc(score_n, 1)
                dve.wait_ge(zm_n, i.q + 1)
                dve.scalar_tensor_tensor(out=mrow[:], in0=zm[:], scalar=SLOPE, in1=zm[:],
                                         op0=ALU.mult, op1=ALU.max).then_inc(mrow_n, 1)

            def minus_max(i):
                dve.wait_ge(mrow_n, i.q + 1)
                dve.tensor_scalar(negm[:], mrow[:], -1.0, None, ALU.mult).then_inc(negm_n, 1)

            def attend(i):
                dve.wait_ge(exp_n, GG * (i.q + 1))
                dve.reciprocal(rden[:], den[:]).then_inc(rden_n, 1)
                dve.wait_ge(rden_n, i.q + 1)
                for g in range(GG):
                    if g % 2 == 0:
                        dve.wait_ge(agg_n, 2 * i.q + g // 2 + 1)
                    dve.scalar_tensor_tensor(out=xs[:, i.r, g], in0=acc[g // 2][:, (g % 2) * D:(g % 2 + 1) * D],
                                             scalar=rden[:, g:g + 1], in1=xs[:, i.r, g],
                                             op0=ALU.mult, op1=ALU.add).then_inc(y1_n, 1)

            def norm1(i):
                dve.wait_ge(rstd_n["1"], i.q + 1)
                for g in range(GG):
                    dve.tensor_scalar(xs[:, i.r, g], xs[:, i.r, g], mv["1"][:, g, 0:1], rstd["1"][:, g:g + 1],
                                      ALU.subtract, ALU.mult).then_inc(z1_n, 1)

            def h_low(i, f):
                for m in range(KD):
                    dve.wait_ge(hthi_n, KD * i.q + m + 1)
                    if f and m == 0:
                        dve.wait_ge(ffn1_n, C * (f.q + 1))
                    dve.tensor_tensor(ht_lo[:, m], ht32[:, i.r, m], ht_hi[:, m].bitcast(F32),
                                      ALU.subtract).then_inc(htlo_n, 1)

            def slot(s, at):
                f, t, b, a = at(0), at(-1), at(1), at(2)
                x0 = at(3) if at(3) and at(3).l == 0 else None
                p = at(4) if at(4) and at(4).l == 0 else None
                if s == -3:
                    dve.wait_ge(vec_turned, 1)
                    dve.tensor_copy(vec[:], sbank[:, 0:NV]).then_inc(vec_ready, 1)
                if t: residual(t)
                if x0:
                    wait(dve, x0_n, GG * x0.g)
                    minus_mean("0", x0.g)
                if a: node_dots(a)
                if b:
                    attend(b)
                    moments("1", b.q, lambda g: xs[:, b.r, g], y1_n)
                if t:
                    moments("2", t.q, lambda g: turn[g // 2][:, (g % 2) * D:(g % 2 + 1) * D], ytok_n, 2)
                if f: split(f, 0)
                if b: variance("1", b.q)
                if t: variance("2", t.q)
                if a: penalty(a)
                if f: split(f, 1)
                if b: norm1(b)
                if t: minus_mean("2", t.q)
                if a: add_bias(a)
                if f: split(f, 2)
                if a: masked(a)
                if f: split(f, 3)
                if a: row_max(a)
                if f: split(f, 4)
                if a: add_si(a)
                if f: split(f, 5)
                if a: leaky(a)
                if f: split(f, 6)
                if a: minus_max(a)
                if f: split(f, 7)
                split_weights(halves_of_slot(s))
                if p:
                    dve.wait_ge(raw(p)[1], raw(p)[2])
                    moments("0", p.g, lambda g: raw(p)[0][:, g])
                if b: h_low(b, f)
                if p: variance("0", p.g)

            for_all_slots(dve, slot, -4)

        @block.scalar
        def _(act):
            def round_weights(ns):
                for n in ns:
                    act.wait_ge(w_in[n % 2], 16 * (n // 2 + 1))
                    act.copy(half_on_chip((w1hi, w2hi), *halves[n]), half_staged(n, halves[n][1])).then_inc(w_hi, 1)

            def gelu(i, c):
                act.wait_ge(ffn1_n, C * i.q + c + 1)
                wait(act, lo_n, C * i.q + c - GRING + 1)
                act.activation(gel[:, c % GRING], hbank[c % HBANKS][:], ACT.Gelu, bias=b1c(i.l, c)).then_inc(gelu_n, 1)

            def high(i, c):
                act.wait_ge(gelu_n, C * i.q + c + 1)
                if c < HRING:
                    wait(act, ffn2_n, C * i.q)
                else:
                    act.wait_ge(ffn2_n, C * i.q + c - HRING + 1)
                act.copy(hid_hi[:, c % HRING], gel[:, c % GRING]).then_inc(hi_n, 1)

            def norm2(i, f):
                t = xs[:, (i.r + 1) % RING] if i.l < L - 1 else xout
                act.wait_ge(nmr_n["2"], i.q + 1)
                if f and i.l < L - 1:
                    act.wait_ge(zt_n, KD * (f.q + 1))
                if i.l == L - 1:
                    act.wait_ge(xout_free, 16 * (i.g + 1))
                for g in range(GG):
                    act.activation(t[:, g], turn[g // 2][:, (g % 2) * D:(g % 2 + 1) * D], ACT.Identity,
                                   bias=nmr["2"][:, g:g + 1], scale=rstd["2"][:, g:g + 1]).then_inc(z2_n, 1)

            def h_high(i, f):
                for m in range(KD):
                    act.wait_ge(zt_n, KD * i.q + m + 1)
                    act.activation(ht32[:, i.r, m], zbank[m][:], ACT.Identity, bias=beta1c(i.l, m),
                                   scale=g1c(i.l, m)).then_inc(ht32_n, 1)
                for m in range(KD):
                    act.wait_ge(ht32_n, KD * i.q + m + 1)
                    if f and m == 0:
                        act.wait_ge(ffn1_n, C * (f.q + 1))
                    act.copy(ht_hi[:, m], ht32[:, i.r, m]).then_inc(hthi_n, 1)

            def exps(i):
                act.wait_ge(score_n, i.q + 1)
                act.wait_ge(negm_n, i.q + 1)
                wait(act, et_n, i.q)
                wait(act, rden_n, i.q)
                for g in range(GG):
                    act.activation(E[:, g], sc[:, g], ACT.Exp, bias=negm[:, g:g + 1],
                                   accum_out=den[:, g:g + 1]).then_inc(exp_n, 1)

            def gelu_table(i):
                wait(act, warm_n, i.q)
                act.activation(warm[:, 1:2], warm[:, 0:1], ACT.Gelu).then_inc(warm_n, 1)

            def et_out(i):
                act.wait_ge(et_n, i.q + 1)
                wait(act, agg_n, 2 * i.q)
                act.copy(ET[:].rearrange("p g j -> p (g j)"), sbank[:]).then_inc(et_sb, 1)

            def first_x(i, f):
                act.wait_ge(nmr_n["0"], i.g + 1)
                if f:
                    act.wait_ge(zt_n, KD * (f.q + 1))
                for g in range(GG):
                    act.activation(xs[:, i.r, g], raw(i)[0][:, g], ACT.Relu, bias=nmr["0"][:, g:g + 1],
                                   scale=rstd["0"][:, g:g + 1]).then_inc(x0_n, 1)

            def slot(s, at):
                f, t, b, a = at(0), at(-1), at(1), at(2)
                p = at(3) if at(3) and at(3).l == 0 else None
                if s == -1:
                    act.wait_ge(vec_ready, 1)
                if s == 0:
                    act.wait_ge(x0_n, GG * (1 + EARLY))
                if f:
                    gelu(f, 0)
                    gelu(f, 1)
                    high(f, 0)
                if p: first_x(p, f)
                round_weights(halves_of_slot(s))
                if f:
                    for c in range(2, C):
                        gelu(f, c)
                        high(f, c - 1)
                if t: norm2(t, f)
                if f: high(f, 7)
                if b: h_high(b, f)
                if a: exps(a)
                if a:
                    gelu_table(a)
                    et_out(a)

            for_all_slots(act, slot, -4)

        @block.tensor
        def _(pe):
            pe.wait_ge(vec_in, 16 * 4)
            pe.wait_ge(const_set, 6)
            pe.transpose(sbank[:, 0:NV], vec_rows[:], ident[0:NV, 0:NV]).then_inc(vec_turned, 1)

            def ffn1(i, c):
                if c == 0:
                    pe.wait_ge(htlo_n, KD * (i.q + 1))
                wait(pe, gelu_n, C * i.q + max(c - HBANKS + 1, 0))
                at_c = slice(c * P, (c + 1) * P)
                for k in range(KD):
                    for n, (w, v) in enumerate(((w1hi, ht_hi), (w1hi, ht_lo), (w1lo, ht_hi))):
                        mm = pe.matmul(hbank[c % HBANKS][:], w[:, i.l, k, at_c], v[:, k],
                                       start=k == 0 and n == 0, stop=k == KD - 1 and n == 2)
                mm.then_inc(ffn1_n, 1)

            def ffn2(i, c):
                pe.wait_ge(lo_n, C * i.q + c + 1)
                for n, (w, v) in enumerate(((w2hi, hid_hi), (w2hi, hid_lo), (w2lo, hid_hi))):
                    for m in range(KD):
                        mm = pe.matmul(acc[m][:], w[:, i.l, c, m * P:(m + 1) * P], v[:, c % HRING],
                                       start=c == 0 and n == 0, stop=c == C - 1 and n == 2)
                mm.then_inc(ffn2_n, 1)

            def aggregate(i, t):
                if t:
                    pe.wait_ge(y2t_n, KD * (t.q + 1))
                pe.wait_ge(et_sb, i.q + 1)
                for g in range(GG):
                    mm = pe.matmul(acc[g // 2][:, (g % 2) * D:(g % 2 + 1) * D], ET[:, g], xs[:, i.r, g],
                                   start=True, stop=True)
                    if g % 2:
                        mm.then_inc(agg_n, 1)

            def y2_back(i):
                pe.wait_ge(y2t_n, KD * (i.q + 1))
                wait(pe, z2_n, GG * i.q)
                for g in range(GG):
                    for m in range(KD):
                        mm = pe.transpose(turn[g // 2][:, (g % 2) * D + m * P:(g % 2) * D + (m + 1) * P],
                                          y2t[:, m, g * P:(g + 1) * P], ident[:])
                    if g % 2:
                        mm.then_inc(ytok_n, 1)

            def sj_rows(i):
                pe.wait_ge(dots_n, i.q + 1)
                if is_item(i, 0, 0):
                    pe.wait_ge(vec_ready, 1)
                wait(pe, et_sb, i.q)
                for g in range(GG):
                    mm = pe.transpose(sbank[:, g * P:(g + 1) * P], dots[:, 1, g:g + 1].to_broadcast([P, P]), ident[:])
                mm.then_inc(sjb_n, 1)

            def z1_turn(i):
                pe.wait_ge(z1_n, GG * (i.q + 1))
                wait(pe, gelu_n, C * i.q - 1)
                wait(pe, ht32_n, KD * i.q)
                for m in range(KD):
                    for g in range(GG):
                        mm = pe.transpose(zbank[m][:, g * P:(g + 1) * P], xs[:, i.r, g, m * P:(m + 1) * P], ident[:])
                    mm.then_inc(zt_n, 1)

            def e_turn(i):
                pe.wait_ge(exp_n, GG * (i.q + 1))
                for g in range(GG):
                    mm = pe.transpose(sbank[:, g * P:(g + 1) * P], E[:, g], ident[:])
                mm.then_inc(et_n, 1)

            def slot(s, at):
                f, t, b, a = at(0), at(-1), at(1), at(2)
                if s in range(0, ROUND, BATCH):
                    pe.wait_ge(w_lo, 4 * (f.l + 1))
                if f:
                    ffn1(f, 0)
                    if s == 0: e_turn(b)
                    ffn1(f, 1)
                if b: aggregate(b, t)
                if t: y2_back(t)
                if f:
                    for c in range(2, 6):
                        ffn1(f, c)
                if a: sj_rows(a)
                if f:
                    ffn1(f, 6)
                    ffn1(f, 7)
                    if b:
                        pe.wait_ge(y1_n, GG * (b.q + 1))
                    elif t:
                        pe.wait_ge(y2t_n, KD * (t.q + 1))
                    ffn2(f, 0)
                    ffn2(f, 1)
                if b: z1_turn(b)
                if f:
                    for c in range(2, C):
                        ffn2(f, c)
                if a and s != -1: e_turn(a)

            for_all_slots(pe, slot, -4)


_INS = ["x", "adj"] + ["L0_gnn_" + n for n in
                       ("attn_w", "attn_b", "W1", "b1", "W2", "b2", "g1", "beta1", "g2", "beta2")]


def kernel(**inputs):
    import numpy as np
    import concourse.bacc as bacc
    from concourse.bass_utils import run_bass_kernel_spmd as run

    nc = bacc.Bacc("TRN2", target_bir_lowering=False, num_devices=1)
    arrays, args = {}, []
    for name in _INS:
        a = np.ascontiguousarray(inputs[name])
        arrays[f"in_{name}_dram"] = a
        args.append(nc.dram_tensor(f"in_{name}_dram", a.shape, mybir.dt.from_np(a.dtype), kind="ExternalInput").ap())
    shape = arrays["in_x_dram"].shape
    args.append(nc.dram_tensor("out_dram", shape, F32, kind="ExternalOutput").ap())
    build(nc, *args)
    return run(nc, [arrays], core_ids=[0]).results[0]["out_dram"]
```

```python
from collections import namedtuple
from contextlib import ExitStack

import concourse.bass as bass
from concourse import mybir

F32 = mybir.dt.float32
F32R = mybir.dt.float32r
I32 = mybir.dt.int32
ALU = mybir.AluOpType
ACT = mybir.ActivationFunctionType
AX_X = mybir.AxisListType.X

P = 128
GG = 4
TOK = GG * P
EPS = 1e-5
SLOPE = 0.2
BIG = 1e30
BATCH = 4
LOOP_FROM, LOOP_TO = 8, 44
RING = 3
HRING = 4
GRING = 3
POOL_SPLITS = 3
HBANKS = 2

Item = namedtuple("Item", "q l g r odd nth")


def build(nc, x, adj, attn_w, attn_b, W1, b1, W2, b2, g1, beta1, g2, beta2, out):
    G, N, D = x.shape
    L, _, H = W1.shape
    assert N == P and D == 2 * P and G % GG == 0
    NG = G // GG
    KD = D // P
    C = H // P
    ROUND = BATCH * L
    ITEMS = NG * L
    EARLY = 2
    assert NG % BATCH == 0 and ROUND % RING == 0 and LOOP_TO + 4 <= ITEMS
    assert (LOOP_TO - LOOP_FROM) % ROUND == 0

    def item(s, k=0):
        if not 0 <= s < ITEMS:
            return None
        return Item(k * ROUND + s, s % ROUND // BATCH, k * BATCH + (s // ROUND * BATCH + s % BATCH),
                    s % RING, s % 2, k * (ROUND // 2) + s // 2)

    def is_item(i, first, last):
        return isinstance(i.q, int) and first <= i.q <= last

    def for_all_slots(eng, slot, first):
        for s in range(first, LOOP_FROM):
            slot(s, lambda d: item(s + d))
        with eng.Fori(0, (LOOP_TO - LOOP_FROM) // ROUND) as k:
            for s in range(LOOP_FROM, LOOP_FROM + ROUND):
                slot(s, lambda d: item(s + d, k))
        for s in range(LOOP_TO, ITEMS + 1):
            slot(s, lambda d: item(s + d))

    def wait(eng, sem, n):
        if not isinstance(n, int) or n > 0:
            eng.wait_ge(sem, n)

    with ExitStack() as ctx:
        def sb(name, shape, dt=F32):
            return ctx.enter_context(nc.sbuf_tensor(name, shape, dt))

        def sem(name):
            return ctx.enter_context(nc.semaphore(name))

        w1hi = sb("w1hi", [P, L, KD, H], F32R)
        w1lo = sb("w1lo", [P, L, KD, H], F32R)
        w2 = sb("w2", [P, L, C, 2, D], F32R)
        hid_hi = sb("hid_hi", [P, HRING, TOK], F32R)
        hid_lo = sb("hid_lo", [P, HRING, TOK], F32R)
        gel = sb("gel", [P, GRING, TOK])
        ht32 = sb("ht32", [P, KD, TOK])
        ht_hi = sb("ht_hi", [P, KD, TOK], F32R)
        ht_lo = sb("ht_lo", [P, KD, TOK], F32R)
        xs = sb("xs", [P, RING, GG, D])
        hb = sb("hb", [P, 2, GG, D])
        y2 = sb("y2", [P, GG, D])
        stage = sb("stage", [P, 2, H])
        xres = stage[:, 0, :].rearrange("p (g d) -> p g d", g=GG)
        xout = stage[:, 1, :].rearrange("p (g d) -> p g d", g=GG)
        xraw = sb("xraw", [P, GG, D])
        early = [hb[:, i] for i in range(EARLY)]
        adji = sb("adji", [P, 2, GG, P], I32)
        scores = sb("scores", [P, 2, GG * P])
        pen = scores[:, 0].rearrange("p (g j) -> p g j", g=GG)
        sc = scores[:, 1].rearrange("p (g j) -> p g j", g=GG)
        junk = scores[:].rearrange("p a b -> p (a b)").bitcast(mybir.dt.bfloat16).rearrange(
            "p (n d) -> p n d", d=D)
        E = sc
        ET_hi = sb("ET_hi", [P, GG, P], F32R)
        ET_lo = sb("ET_lo", [P, GG, P], F32R)
        x_hi = sb("x_hi", [P, GG, D], F32R)
        x_lo = sb("x_lo", [P, GG, D], F32R)
        ident = sb("ident", [P, P])
        diag = sb("diag", [P, P])
        warm = sb("warm", [P, 2])
        fence = sb("fence", [P, 1])
        pool_fence = sb("pool_fence", [P, 1])
        attn_rows = sb("attn_rows", [P, L, 2, D])
        ln2_rows = sb("ln2_rows", [P, 2, L, D])
        ln1_rows = sb("ln1_rows", [P, 2, L, D])
        attn_bias = sb("attn_bias", [P, L])
        NV = L * (C + 2 * KD)
        vec_rows = scores[0:NV, 0, 0:P]
        vec = sb("vec", [P, NV])
        dots = sb("dots", [P, 2, GG])
        si = sb("si", [P, GG])
        mx = sb("mx", [P, GG])
        zm = sb("zm", [P, GG])
        mrow = sb("mrow", [P, GG])
        negm = sb("negm", [P, GG])
        den = sb("den", [P, GG])
        rden = sb("rden", [P, GG])
        halfs = sb("halfs", [P, GG])
        st = {n: sb(f"st{n}", [P, GG, 6]) for n in "012"}
        mv = {n: sb(f"mv{n}", [P, GG, 2]) for n in "012"}
        ve = {n: sb(f"ve{n}", [P, GG]) for n in "012"}
        rstd = {n: sb(f"rstd{n}", [P, GG]) for n in "012"}
        nmr = {n: sb(f"nmr{n}", [P, GG]) for n in "02"}

        def b1c(l, c): return vec[:, l * C + c:l * C + c + 1]
        def dcol(n, l, m):
            at = L * C + (n * L + l) * KD + m
            return vec[:, at:at + 1]
        def g1c(l, m): return dcol(0, l, m)
        def beta1c(l, m): return dcol(1, l, m)

        hbank = [ctx.enter_context(nc.psum_tensor(f"hbank{i}", [P, TOK], F32)) for i in range(HBANKS)]
        acc = [ctx.enter_context(nc.psum_tensor(f"acc{g}", [P, 2, D], F32)) for g in range(GG)]
        zbank = ctx.enter_context(nc.psum_tensor("zbank", [P, TOK], F32))
        sbank = ctx.enter_context(nc.psum_tensor("sbank", [P, TOK], F32))

        vec_in = sem("vec_in")
        attn_in = sem("attn_in")
        ln1_in = sem("ln1_in")
        ln2_in = sem("ln2_in")
        const_set = sem("const_set")
        vec_turned = sem("vec_turned")
        vec_ready = sem("vec_ready")
        w_in = [sem(f"w_in{i}") for i in range(2)]
        w_hi = sem("w_hi")
        w_lo = sem("w_lo")
        adj_in = [sem(f"adj_in{r}") for r in range(2)]
        early_in = [sem(f"early_in{i}") for i in range(EARLY)]
        xraw_in = sem("xraw_in")
        xres_in = sem("xres_in")
        xout_free = sem("xout_free")
        ffn1_n = sem("ffn1_n")
        ffn2_n = sem("ffn2_n")
        agg_n = sem("agg_n")
        sjb_n = sem("sjb_n")
        et_n = sem("et_n")
        zt_n = sem("zt_n")
        et_lo = sem("et_lo")
        y2a_n = sem("y2a_n")
        y2_n = sem("y2_n")
        pen_n = sem("pen_n")
        dots_n = sem("dots_n")
        si_n = sem("si_n")
        mask_n = sem("mask_n")
        mx_n = sem("mx_n")
        zm_n = sem("zm_n")
        mrow_n = sem("mrow_n")
        negm_n = sem("negm_n")
        z_n = sem("z_n")
        score_n = sem("score_n")
        rden_n = sem("rden_n")
        y1_n = sem("y1_n")
        z1_n = sem("z1_n")
        htlo_n = sem("htlo_n")
        st_n = {n: sem(f"st{n}_n") for n in "012"}
        mv_n = {n: sem(f"mv{n}_n") for n in "012"}
        ve_n = {n: sem(f"ve{n}_n") for n in "012"}
        nmr_n = {n: sem(f"nmr{n}_n") for n in "02"}
        lo_dve = sem("lo_dve")
        gelu_n = sem("gelu_n")
        hi_n = sem("hi_n")
        z2_n = sem("z2_n")
        ht32_n = sem("ht32_n")
        hthi_n = sem("hthi_n")
        exp_n = sem("exp_n")
        warm_n = sem("warm_n")
        et_hi = sem("et_hi")
        xhi_n = sem("xhi_n")
        x0_n = sem("x0_n")
        rstd_n = {n: sem(f"rstd{n}_n") for n in "012"}
        xlo_n = sem("xlo_n")
        lo_pool = sem("lo_pool")
        ln1_ready = sem("ln1_ready")
        hgam_n = sem("hgam_n")
        hb_n = sem("hb_n")
        gam_n = sem("gam_n")
        x_n = sem("x_n")
        out_ready = sem("out_ready")

        block = ctx.enter_context(nc.Block())

        def group(t, g):
            return t.rearrange("(n g) p d -> n p g d", g=GG)[g]

        def raw(i):
            if is_item(i, 1, EARLY):
                return early[i.q - 1], early_in[i.q - 1], 16
            return xraw, xraw_in, 16 * (i.g + 1 if is_item(i, 0, 0) else i.g + 1 - EARLY)

        halves = [(l, w, h) for l in range(L) for w in range(2) for h in range(2)]

        def halves_of_slot(s):
            if s in (-3, -1):
                return range(s + 3, s + 5)
            return range(s + 4, s + 5) if 0 <= s < 4 * (L - 1) else ()

        def half_in_dram(l, w, h):
            if w == 0:
                return W1[l, h * P:(h + 1) * P, :]
            return W2[l].rearrange("(h c p) d -> h p c d", h=2, p=P)[h]

        def half_on_chip(low, l, w, h):
            return (w1hi, w1lo)[low][:, l, h, :] if w == 0 else w2[:, l, h * (C // 2):(h + 1) * (C // 2), low]

        def half_staged(n, w):
            t = stage[:, n % 2, :]
            return t if w == 0 else t.rearrange("p (c d) -> p c d", d=D)

        def wait_x(eng, i):
            if i.l == 0:
                eng.wait_ge(x0_n, GG * (i.g + 1))
            else:
                eng.wait_ge(x_n, i.q - BATCH + 1)

        def wait_lo(eng, q, c):
            if c < POOL_SPLITS:
                wait(eng, lo_pool, POOL_SPLITS * q + c + 1)
            else:
                wait(eng, lo_dve, (C - POOL_SPLITS) * q + c - POOL_SPLITS + 1)

        def high(eng, i, c):
            eng.wait_ge(gelu_n, C * i.q + c + 1)
            if c < HRING:
                wait(eng, ffn2_n, C * i.q)
            else:
                eng.wait_ge(ffn2_n, C * i.q + c - HRING + 1)
            copy = eng.tensor_copy if c == C - 1 else eng.copy
            copy(hid_hi[:, c % HRING], gel[:, c % GRING]).then_inc(hi_n, 1)

        def split(eng, i, c):
            hi, lo, g32 = hid_hi[:, c % HRING], hid_lo[:, c % HRING], gel[:, c % GRING]
            if c >= HRING:
                eng.wait_ge(ffn2_n, C * i.q + c - HRING + 1)
            eng.wait_ge(hi_n, C * i.q + c + 1)
            eng.tensor_tensor(lo, g32, hi.bitcast(F32), ALU.subtract).then_inc(
                lo_pool if c < POOL_SPLITS else lo_dve, 1)

        def next_x(eng, i):
            t = xs[:, (i.r + 1) % RING] if i.l < L - 1 else xout
            if is_item(i, 0, 0):
                eng.wait_ge(ln2_in, 16 * 2)
            eng.wait_ge(z2_n, GG * (i.q + 1))
            eng.tensor_tensor(t, t, ln2_rows[:, 0, i.l].unsqueeze(1).to_broadcast([P, GG, D]),
                              ALU.mult).then_inc(gam_n, 1)
            eng.wait_ge(gam_n, i.q + 1)
            eng.tensor_tensor(t, t, ln2_rows[:, 1, i.l].unsqueeze(1).to_broadcast([P, GG, D]),
                              ALU.add).then_inc(x_n, 1)

        def add_input(eng, i):
            eng.wait_ge(x_n, i.q + 1)
            eng.wait_ge(xres_in, 16 * (i.g + 1))
            eng.tensor_tensor(xout, xout, xres, ALU.add).then_inc(out_ready, 1)

        @block.sync
        def _(sp):
            def load_small():
                rows = 0
                for t, pieces in ((b1, C), (g1, KD), (beta1, KD)):
                    n = L * pieces
                    sp.dma_start(vec_rows[rows:rows + n, :], t.rearrange("l (c p) -> (l c) p", p=P)).then_inc(vec_in, 16)
                    rows += n
                sp.dma_start(attn_rows[:], attn_w.rearrange("l (t d) -> l t d", t=2).partition_broadcast(P)).then_inc(attn_in, 16)
                sp.dma_start(attn_bias[:], attn_b.partition_broadcast(P)).then_inc(attn_in, 16)

            def load_ln1_rows():
                sp.dma_start(ln1_rows[:, 0], g1.partition_broadcast(P)).then_inc(ln1_in, 16)
                sp.dma_start(ln1_rows[:, 1], beta1.partition_broadcast(P)).then_inc(ln1_in, 16)
                sp.dma_start(y2[:, 0:L], b2.partition_broadcast(P)).then_inc(ln1_in, 16)

            def load_ln2_rows():
                sp.dma_start(ln2_rows[:, 0], g2.partition_broadcast(P)).then_inc(ln2_in, 16)
                sp.dma_start(ln2_rows[:, 1], beta2.partition_broadcast(P)).then_inc(ln2_in, 16)

            def load_xraw(i):
                t, arrived, _ = raw(i)
                if t is xraw:
                    wait(sp, x0_n, GG * (1 if is_item(i, 1 + EARLY, 1 + EARLY) else i.g))
                sp.dma_start(t[:], group(x, i.g)).then_inc(arrived, 16)

            def load_adj(i):
                wait(sp, pen_n, i.q - 1)
                sp.dma_start(adji[:, i.odd], group(adj, i.g)).then_inc(adj_in[i.odd], 16)

            def load_weights(n):
                l, w, h = halves[n]
                wait(sp, w_lo, n - 1)
                sp.dma_start(half_staged(n, w), half_in_dram(l, w, h)).then_inc(w_in[n % 2], 16)

            def slot(s, at):
                if at(4) and at(4).l == 0:
                    load_xraw(at(4))
                if s == -4:
                    load_small()
                if at(3):
                    load_adj(at(3))
                for n in halves_of_slot(s + 1):
                    load_weights(n)
                if s == -3:
                    load_ln1_rows()
                if s == -1:
                    load_ln2_rows()
                if at(-1) and at(-1).l == L - 1:
                    wait(sp, out_ready, at(-1).g + 1)
                    sp.dma_start(group(out, at(-1).g), xout).then_inc(xout_free, 16)
                if at(0) and at(0).l == L - 1:
                    sp.dma_start(xres, group(x, at(0).g)).then_inc(xres_in, 16)

            for_all_slots(sp, slot, -4)
            sp.wait_ge(xout_free, 16 * (NG + 1))

        @block.gpsimd
        def _(pool):
            pool.memset(ident[:], 0.0).then_inc(const_set, 1)
            pool.memset(diag[:], -BIG).then_inc(const_set, 1)
            pool.memset(halfs[:], -0.5).then_inc(const_set, 1)
            pool.memset(warm[:], 0.0).then_inc(const_set, 1)
            pool.wait_ge(const_set, 4)
            for t, fill in ((ident, 1.0), (diag, BIG)):
                pool.affine_select(out=t[:], in_=t[:], compare_op=ALU.not_equal, fill=fill, base=0,
                                   pattern=[[-1, P]], channel_multiplier=1).then_inc(const_set, 1)
            pool.wait_ge(const_set, 6)

            def make_rstd(n, q):
                pool.wait_ge(ve_n[n], q + 1)
                pool.tensor_tensor(rstd[n][:], ve[n][:], halfs[:], ALU.pow).then_inc(rstd_n[n], 1)

            def h_rows(i):
                if is_item(i, 0, 0):
                    pool.wait_ge(ln1_ready, 1)
                if is_item(i, 0, EARLY - 1):
                    pool.wait_ge(x0_n, GG * (i.q + 2))
                t = hb[:, i.odd]
                pool.wait_ge(z1_n, GG * (i.q + 1))
                wait(pool, y2_n, GG * (i.q - 1))
                pool.tensor_tensor(t, xs[:, i.r], ln1_rows[:, 0, i.l].unsqueeze(1).to_broadcast([P, GG, D]),
                                   ALU.mult).then_inc(hgam_n, 1)
                pool.wait_ge(hgam_n, i.q + 1)
                pool.tensor_tensor(t, t, ln1_rows[:, 1, i.l].unsqueeze(1).to_broadcast([P, GG, D]),
                                   ALU.add).then_inc(hb_n, 1)

            def x_low(i):
                pool.wait_ge(xhi_n, i.q + 1)
                pool.tensor_tensor(x_lo[:], xs[:, i.r], x_hi[:].bitcast(F32), ALU.subtract).then_inc(xlo_n, 1)

            def sum_biases():
                pool.wait_ge(ln1_in, 16 * 3)
                pool.tensor_tensor(ln1_rows[:, 1], ln1_rows[:, 1], y2[:, 0:L], ALU.add).then_inc(ln1_ready, 1)

            def slot(s, at):
                if at(0):
                    for c in range(POOL_SPLITS):
                        split(pool, at(0), c)
                if at(1):
                    wait(pool, z1_n, GG * at(1).q)
                    make_rstd("1", at(1).q)
                if at(-1):
                    wait(pool, z2_n, GG * at(-1).q)
                    make_rstd("2", at(-1).q)
                if at(1): h_rows(at(1))
                if at(2): x_low(at(2))
                if at(-1) and s < ITEMS: next_x(pool, at(-1))
                if s == -2:
                    wait(pool, x0_n, GG * item(1).g)
                    make_rstd("0", item(1).g)
                if at(4) and at(4).l == 0 and s != -3:
                    wait(pool, x0_n, GG * at(4).g)
                    make_rstd("0", at(4).g)
                if at(-1) and at(-1).l == L - 1 and s < ITEMS: add_input(pool, at(-1))
                if s == -2: sum_biases()
                if s == 7:
                    pool.wait_ge(w_lo, len(halves))
                    pool.memset(pool_fence[:], 0.0).then_inc(xout_free, 16)

            for_all_slots(pool, slot, -4)

        @block.vector
        def _(dve):
            def split_weights(ns):
                for n in ns:
                    dve.wait_ge(w_hi, n + 1)
                    dve.tensor_tensor(half_on_chip(1, *halves[n]), half_staged(n, halves[n][1]),
                                      half_on_chip(0, *halves[n]).bitcast(F32),
                                      ALU.subtract).then_inc(w_lo, 1)

            def moments(n, q, src, ready=None):
                for g in range(GG):
                    if ready:
                        dve.wait_ge(ready, GG * q + g + 1)
                    dve.bn_stats(st[n][:, g], src(g)).then_inc(st_n[n], 1)

            def variance(n, q):
                dve.wait_ge(st_n[n], GG * (q + 1))
                dve.memset(fence[:], 0.0)
                for g in range(GG):
                    dve.bn_aggr(mv[n][:, g], st[n][:, g]).then_inc(mv_n[n], 1)
                dve.wait_ge(mv_n[n], GG * (q + 1))
                dve.tensor_scalar(ve[n][:], mv[n][:, :, 1], EPS, None, ALU.add).then_inc(ve_n[n], 1)

            def input_moments(i):
                dve.wait_ge(raw(i)[1], raw(i)[2])
                moments("0", i.g, lambda g: raw(i)[0][:, g])

            def minus_mean(n, q):
                dve.wait_ge(rstd_n[n], q + 1)
                dve.scalar_tensor_tensor(out=nmr[n][:], in0=mv[n][:, :, 0], scalar=-1.0, in1=rstd[n][:],
                                         op0=ALU.mult, op1=ALU.mult).then_inc(nmr_n[n], 1)

            def et_low(i):
                dve.wait_ge(et_hi, i.q + 1)
                dve.tensor_tensor(ET_lo[:].rearrange("p g j -> p (g j)"), sbank[:],
                                  ET_hi[:].rearrange("p g j -> p (g j)").bitcast(F32), ALU.subtract).then_inc(et_lo, 1)

            def residual_upper(i):
                wait(dve, z2_n, GG * i.q)
                dve.wait_ge(hb_n, i.q + 1)
                dve.wait_ge(ffn2_n, C * (i.q + 1))
                for g in range(GG):
                    dve.tensor_tensor(y2[:, g], acc[g][:, 0], hb[:, i.odd, g], ALU.add).then_inc(y2a_n, 1)

            def residual_lower(i):
                for g in range(GG):
                    dve.wait_ge(y2a_n, GG * i.q + g + 1)
                    dve.tensor_tensor(y2[:, g], acc[g][:, 1], y2[:, g], ALU.add).then_inc(y2_n, 1)

            def node_dots(i):
                wait_x(dve, i)
                wait(dve, sjb_n, i.q)
                wait(dve, et_n, i.q)
                if is_item(i, 0, 0):
                    dve.wait_ge(attn_in, 16 * 2)
                for t in (1, 0):
                    for g in range(GG):
                        last = dve.tensor_tensor_reduce(junk[:, GG * t + g], xs[:, i.r, g], attn_rows[:, i.l, t], 1.0, 0.0,
                                                        ALU.mult, ALU.add, dots[:, t, g:g + 1])
                last.then_inc(dots_n, 1)

            def add_bias(i):
                dve.wait_ge(dots_n, i.q + 1)
                dve.tensor_scalar(si[:], dots[:, 0], attn_bias[:, i.l:i.l + 1], None, ALU.add).then_inc(si_n, 1)

            def penalty(i):
                dve.wait_ge(adj_in[i.odd], 16 * (i.nth + 1))
                dve.wait_ge(dots_n, i.q + 1)
                dve.scalar_tensor_tensor(out=pen[:], in0=adji[:, i.odd], scalar=2 * BIG,
                                         in1=diag[:].unsqueeze(1).to_broadcast([P, GG, P]),
                                         op0=ALU.mult, op1=ALU.add).then_inc(pen_n, 1)

            def masked(i):
                dve.wait_ge(pen_n, i.q + 1)
                dve.wait_ge(sjb_n, i.q + 1)
                dve.tensor_tensor(sc[:], pen[:], sbank[:].rearrange("p (g j) -> p g j", g=GG),
                                  ALU.min).then_inc(mask_n, 1)

            def row_max(i):
                dve.wait_ge(mask_n, i.q + 1)
                dve.tensor_reduce(mx[:], sc[:], AX_X, ALU.max).then_inc(mx_n, 1)

            def add_si(i):
                dve.wait_ge(si_n, i.q + 1)
                dve.wait_ge(mx_n, i.q + 1)
                dve.tensor_tensor(sc[:], sc[:], si[:].unsqueeze(2).to_broadcast([P, GG, P]),
                                  ALU.add).then_inc(z_n, 1)
                dve.tensor_tensor(zm[:], mx[:], si[:], ALU.add).then_inc(zm_n, 1)

            def leaky(i):
                dve.wait_ge(z_n, i.q + 1)
                dve.scalar_tensor_tensor(out=sc[:], in0=sc[:], scalar=SLOPE, in1=sc[:],
                                         op0=ALU.mult, op1=ALU.max).then_inc(score_n, 1)
                dve.wait_ge(zm_n, i.q + 1)
                dve.scalar_tensor_tensor(out=mrow[:], in0=zm[:], scalar=SLOPE, in1=zm[:],
                                         op0=ALU.mult, op1=ALU.max).then_inc(mrow_n, 1)

            def minus_max(i):
                dve.wait_ge(mrow_n, i.q + 1)
                dve.tensor_scalar(negm[:], mrow[:], -1.0, None, ALU.mult).then_inc(negm_n, 1)

            def attend(i):
                dve.wait_ge(exp_n, GG * (i.q + 1))
                dve.reciprocal(rden[:], den[:]).then_inc(rden_n, 1)
                dve.wait_ge(rden_n, i.q + 1)
                for g in range(GG):
                    if g % 2 == 0:
                        dve.wait_ge(agg_n, 2 * i.q + g // 2 + 1)
                    dve.scalar_tensor_tensor(out=xs[:, i.r, g], in0=acc[g][:, 0],
                                             scalar=rden[:, g:g + 1], in1=xs[:, i.r, g],
                                             op0=ALU.mult, op1=ALU.add).then_inc(y1_n, 1)

            def norm1(i):
                dve.wait_ge(rstd_n["1"], i.q + 1)
                for g in range(GG):
                    dve.tensor_scalar(xs[:, i.r, g], xs[:, i.r, g], mv["1"][:, g, 0:1], rstd["1"][:, g:g + 1],
                                      ALU.subtract, ALU.mult).then_inc(z1_n, 1)

            def h_low(i, f):
                for m in range(KD):
                    dve.wait_ge(hthi_n, KD * i.q + m + 1)
                    if f and m == 0:
                        dve.wait_ge(ffn1_n, C * (f.q + 1))
                    dve.tensor_tensor(ht_lo[:, m], ht32[:, m], ht_hi[:, m].bitcast(F32),
                                      ALU.subtract).then_inc(htlo_n, 1)

            def slot(s, at):
                f, t, b, a = at(0), at(-1), at(1), at(2)
                x0 = at(3) if at(3) and at(3).l == 0 else None
                p = at(4) if at(4) and at(4).l == 0 else None
                if s == -3:
                    dve.wait_ge(vec_turned, 1)
                    dve.tensor_copy(vec[:], sbank[:, 0:NV]).then_inc(vec_ready, 1)
                if t: residual_upper(t)
                if b: et_low(b)
                if t: residual_lower(t)
                if x0 and s != -2:
                    wait(dve, x0_n, GG * x0.g)
                    minus_mean("0", x0.g)
                if a: node_dots(a)
                if b:
                    attend(b)
                    moments("1", b.q, lambda g: xs[:, b.r, g], y1_n)
                    variance("1", b.q)
                if t: moments("2", t.q, lambda g: y2[:, g], y2_n)
                if b: norm1(b)
                if f: split(dve, f, 3)
                if t:
                    variance("2", t.q)
                if f: split(dve, f, 4)
                if t: minus_mean("2", t.q)
                if a: penalty(a)
                if a: add_bias(a)
                if a: masked(a)
                if f: split(dve, f, 5)
                if a: row_max(a)
                if a: add_si(a)
                if f: split(dve, f, 6)
                if a: leaky(a)
                if a: minus_max(a)
                if f:
                    high(dve, f, 7)
                    split(dve, f, 7)
                if s == -2:
                    input_moments(item(1))
                    variance("0", item(1).g)
                    wait(dve, x0_n, GG * item(1).g)
                    minus_mean("0", item(1).g)
                    split_weights(halves_of_slot(-3))
                if s != -3:
                    if s != -1: split_weights(halves_of_slot(s))
                    if p and s != -1: input_moments(p)
                if b: h_low(b, f)
                if s == -1:
                    split_weights(halves_of_slot(s))
                    input_moments(p)
                if p and s != -3: variance("0", p.g)
                if s == ITEMS:
                    next_x(dve, t)
                    add_input(dve, t)

            for_all_slots(dve, slot, -4)

        @block.scalar
        def _(act):
            def round_weights(ns):
                for n in ns:
                    act.wait_ge(w_in[n % 2], 16 * (n // 2 + 1))
                    act.copy(half_on_chip(0, *halves[n]), half_staged(n, halves[n][1])).then_inc(w_hi, 1)

            def gelu(i, c):
                act.wait_ge(ffn1_n, C * i.q + c + 1)
                if c < GRING:
                    wait_lo(act, i.q - 1, c + C - GRING)
                else:
                    wait_lo(act, i.q, c - GRING)
                act.activation(gel[:, c % GRING], hbank[c % HBANKS][:], ACT.Gelu, bias=b1c(i.l, c)).then_inc(gelu_n, 1)

            def norm2(i, f):
                t = xs[:, (i.r + 1) % RING] if i.l < L - 1 else xout
                act.wait_ge(nmr_n["2"], i.q + 1)
                if f and i.l < L - 1:
                    act.wait_ge(zt_n, KD * (f.q + 1))
                if i.l == L - 1:
                    act.wait_ge(xout_free, 16 * (i.g + 1))
                for g in range(GG):
                    act.activation(t[:, g], y2[:, g], ACT.Identity,
                                   bias=nmr["2"][:, g:g + 1], scale=rstd["2"][:, g:g + 1]).then_inc(z2_n, 1)

            def h_out(i, m):
                act.wait_ge(zt_n, KD * i.q + m + 1)
                if m == 0:
                    wait(act, htlo_n, KD * i.q)
                act.activation(ht32[:, m], zbank[:], ACT.Identity, bias=beta1c(i.l, m),
                               scale=g1c(i.l, m)).then_inc(ht32_n, 1)

            def h_high(i, f):
                for m in range(KD):
                    act.wait_ge(ht32_n, KD * i.q + m + 1)
                    if f and m == 0:
                        act.wait_ge(ffn1_n, C * (f.q + 1))
                    act.copy(ht_hi[:, m], ht32[:, m]).then_inc(hthi_n, 1)

            def exps(i):
                act.wait_ge(score_n, i.q + 1)
                act.wait_ge(negm_n, i.q + 1)
                wait(act, rden_n, i.q)
                for g in range(GG):
                    act.activation(E[:, g], sc[:, g], ACT.Exp, bias=negm[:, g:g + 1],
                                   accum_out=den[:, g:g + 1]).then_inc(exp_n, 1)

            def gelu_table(i):
                wait(act, warm_n, i.q)
                act.activation(warm[:, 1:2], warm[:, 0:1], ACT.Gelu).then_inc(warm_n, 1)

            def et_out(i):
                act.wait_ge(et_n, i.q + 1)
                wait(act, agg_n, 2 * i.q)
                act.copy(ET_hi[:].rearrange("p g j -> p (g j)"), sbank[:]).then_inc(et_hi, 1)

            def x_high(i, before):
                wait_x(act, i)
                if before:
                    act.wait_ge(agg_n, 2 * (before.q + 1))
                act.copy(x_hi[:], xs[:, i.r]).then_inc(xhi_n, 1)

            def first_x(i, f):
                act.wait_ge(nmr_n["0"], i.g + 1)
                if f:
                    act.wait_ge(zt_n, KD * (f.q + 1))
                for g in range(GG):
                    act.activation(xs[:, i.r, g], raw(i)[0][:, g], ACT.Relu, bias=nmr["0"][:, g:g + 1],
                                   scale=rstd["0"][:, g:g + 1]).then_inc(x0_n, 1)

            def slot(s, at):
                f, t, b, a = at(0), at(-1), at(1), at(2)
                p = at(3) if at(3) and at(3).l == 0 else None
                if s == -1:
                    act.wait_ge(vec_ready, 1)
                if f:
                    gelu(f, 0)
                    gelu(f, 1)
                    high(act, f, 0)
                if p and s != -2: first_x(p, f)
                round_weights(halves_of_slot(s))
                if f:
                    gelu(f, 2)
                    high(act, f, 1)
                    gelu(f, 3)
                    high(act, f, 2)
                if a: x_high(a, b)
                if f:
                    for c in (4, 5, 6):
                        gelu(f, c)
                        high(act, f, c - 1)
                if b: h_out(b, 0)
                if t: norm2(t, f)
                if f:
                    gelu(f, 7)
                    high(act, f, 6)
                if b:
                    h_out(b, 1)
                    h_high(b, f)
                if a:
                    exps(a)
                    et_out(a)
                    gelu_table(a)
                if s == -2: first_x(p, f)

            for_all_slots(act, slot, -4)

        @block.tensor
        def _(pe):
            pe.wait_ge(vec_in, 16 * 3)
            pe.wait_ge(const_set, 6)
            pe.transpose(sbank[:, 0:NV], vec_rows, ident[0:NV, 0:NV]).then_inc(vec_turned, 1)

            def ffn1(i, c):
                if c == 0:
                    pe.wait_ge(htlo_n, KD * (i.q + 1))
                wait(pe, gelu_n, C * i.q + max(c - HBANKS + 1, 0))
                at_c = slice(c * P, (c + 1) * P)
                for k in range(KD):
                    for n, (w, v) in enumerate(((w1hi, ht_hi), (w1hi, ht_lo), (w1lo, ht_hi))):
                        mm = pe.matmul(hbank[c % HBANKS][:], w[:, i.l, k, at_c], v[:, k],
                                       start=k == 0 and n == 0, stop=k == KD - 1 and n == 2)
                mm.then_inc(ffn1_n, 1)

            def ffn2(i, c):
                wait_lo(pe, i.q, c)
                for g in range(GG):
                    of_g = slice(g * P, (g + 1) * P)
                    pe.matmul(acc[g][:].rearrange("p t d -> p (t d)"), hid_hi[:, c % HRING, of_g],
                              w2[:, i.l, c].rearrange("p t d -> p (t d)"), start=c == 0, stop=False)
                    mm = pe.matmul(acc[g][:, 0], hid_lo[:, c % HRING, of_g], w2[:, i.l, c, 0],
                                   start=False, stop=c == C - 1)
                mm.then_inc(ffn2_n, 1)

            def aggregate(i, t):
                pe.wait_ge(et_lo, i.q + 1)
                pe.wait_ge(xlo_n, i.q + 1)
                for g in range(GG):
                    if t:
                        pe.wait_ge(y2_n, GG * t.q + g + 1)
                    for n, (w, v) in enumerate(((ET_hi, x_hi), (ET_hi, x_lo), (ET_lo, x_hi))):
                        mm = pe.matmul(acc[g][:, 0], w[:, g], v[:, g], start=n == 0, stop=n == 2)
                    if g % 2:
                        mm.then_inc(agg_n, 1)

            def sj_rows(i):
                pe.wait_ge(dots_n, i.q + 1)
                if is_item(i, 0, 0):
                    pe.wait_ge(vec_ready, 1)
                wait(pe, et_lo, i.q)
                for g in range(GG):
                    mm = pe.transpose(sbank[:, g * P:(g + 1) * P], dots[:, 1, g:g + 1].to_broadcast([P, P]), ident[:])
                mm.then_inc(sjb_n, 1)

            def z1_turn(i, m):
                pe.wait_ge(z1_n, GG * (i.q + 1))
                wait(pe, ht32_n, KD * i.q + m)
                for g in range(GG):
                    mm = pe.transpose(zbank[:, g * P:(g + 1) * P], xs[:, i.r, g, m * P:(m + 1) * P], ident[:])
                mm.then_inc(zt_n, 1)

            def e_turn(i):
                pe.wait_ge(exp_n, GG * (i.q + 1))
                for g in range(GG):
                    mm = pe.transpose(sbank[:, g * P:(g + 1) * P], E[:, g], ident[:])
                mm.then_inc(et_n, 1)

            def slot(s, at):
                f, t, b, a = at(0), at(-1), at(1), at(2)
                if s in range(0, ROUND, BATCH):
                    pe.wait_ge(w_lo, 4 * f.l + 2 if s == 0 else 4 * (f.l + 1))
                if f:
                    ffn1(f, 0)
                    if s == 0: e_turn(b)
                    ffn1(f, 1)
                if b: aggregate(b, t)
                if f:
                    ffn1(f, 2)
                    ffn1(f, 3)
                if a: sj_rows(a)
                if f:
                    ffn1(f, 4)
                    ffn1(f, 5)
                    if s == 0:
                        pe.wait_ge(w_lo, 4)
                    if b:
                        pe.wait_ge(y1_n, GG * (b.q + 1))
                    elif t:
                        pe.wait_ge(y2_n, GG * (t.q + 1))
                    ffn2(f, 0)
                    ffn2(f, 1)
                    ffn1(f, 6)
                if b: z1_turn(b, 0)
                if f:
                    ffn2(f, 2)
                    ffn1(f, 7)
                if b: z1_turn(b, 1)
                if f:
                    for c in range(3, C):
                        ffn2(f, c)
                if a and s != -1: e_turn(a)

            for_all_slots(pe, slot, -4)


_INS = ["x", "adj"] + ["L0_gnn_" + n for n in
                       ("attn_w", "attn_b", "W1", "b1", "W2", "b2", "g1", "beta1", "g2", "beta2")]


def kernel(**inputs):
    import numpy as np
    import concourse.bacc as bacc
    from concourse.bass_utils import run_bass_kernel_spmd as run

    nc = bacc.Bacc("TRN2", target_bir_lowering=False, num_devices=1)
    arrays, args = {}, []
    for name in _INS:
        a = np.ascontiguousarray(inputs[name])
        arrays[f"in_{name}_dram"] = a
        args.append(nc.dram_tensor(f"in_{name}_dram", a.shape, mybir.dt.from_np(a.dtype), kind="ExternalInput").ap())
    shape = arrays["in_x_dram"].shape
    args.append(nc.dram_tensor("out_dram", shape, F32, kind="ExternalOutput").ap())
    build(nc, *args)
    return run(nc, [arrays], core_ids=[0]).results[0]["out_dram"]
```
